# Optimizing a Trainium2 kernel written in Bass

```python
import numpy as np
import jax
import jax.numpy as jnp

def _softmax(x, axis=-1):
    return jax.nn.softmax(x, axis=axis)

def _gelu(x):
    return jax.nn.gelu(x, approximate=True)

def _silu(x):
    return jax.nn.silu(x)

def _sigmoid(x):
    return jax.nn.sigmoid(x)

def _layernorm(x, axis=-1, eps=1e-05):
    m = jnp.mean(x, axis=axis, keepdims=True)
    v = jnp.var(x, axis=axis, keepdims=True)
    return (x - m) / jnp.sqrt(v + eps)

def _scatter_add(tgt, idx, src, axis=0):
    return tgt.at[idx].add(src)

def _segment_sum(src, seg, n):
    return jax.ops.segment_sum(src, seg, n)
kernel_name = 'mk_gnn_resnorm_d2_gnn_r8_86385a'

def setup_inputs(seed: int=0):
    np.random.seed(seed)
    _w = jnp.asarray

    def _rec_inputs():
        import jax
        import jax.numpy as jnp
        _gk = jax.random.key(seed)
        x = -0.0003713 + 1 * jax.random.normal(jax.random.fold_in(_gk, 1), (6250, 256), jnp.float32)
        _s = jax.random.randint(jax.random.fold_in(_gk, 2), (50000,), 0, 6250, jnp.int32)
        _d = jax.random.randint(jax.random.fold_in(_gk, 3), (50000,), 0, 6250, jnp.int32)
        _loop = jnp.arange(6250, dtype=jnp.int32)
        src = jnp.concatenate([_s, _d, _loop])
        dst = jnp.concatenate([_d, _s, _loop])
        _o = jnp.argsort(dst, stable=True)
        src = src[_o]
        dst = dst[_o]
        edge_attr_10 = jax.random.uniform(jax.random.fold_in(_gk, 12), (106250, 10), jnp.float32, 0.0, 1)
        edge_attr_4 = 0.00109026 + 0.999989 * jax.random.normal(jax.random.fold_in(_gk, 13), (106250, 4), jnp.float32)
        edge_weight = jax.random.uniform(jax.random.fold_in(_gk, 14), (106250,), jnp.float32, 0.0, 0.999998)
        edge_weight_n2 = jax.random.uniform(jax.random.fold_in(_gk, 15), (106250,), jnp.float32, 0.0, 0.999998)
        return (x, src, dst, edge_attr_10, edge_attr_4, edge_weight, edge_weight_n2)
    x, src, dst, edge_attr_10, edge_attr_4, edge_weight, edge_weight_n2 = _rec_inputs()

    def _L0_gnn_setup():
        import jax, jax.numpy as jnp
        import numpy as np
        MUL = 64
        N_NODES = 6250
        N_EDGES = 100000
        NUM_NEIGHBORS = 16.0
        SILU_NORM = 1.679177
        key = jax.random.key(seed)
        ks = jax.random.split(key, 9)
        node_in = jax.random.normal(ks[0], (N_NODES, 4 * MUL), dtype=jnp.float32)
        edge_src = jax.random.randint(ks[1], (N_EDGES,), 0, N_NODES)
        edge_dst = jax.random.randint(ks[2], (N_EDGES,), 0, N_NODES)
        edge_attr = jax.random.normal(ks[3], (N_EDGES, 4), dtype=jnp.float32)
        edge_len_emb = jax.random.uniform(ks[4], (N_EDGES, 10), dtype=jnp.float32)
        w_00_0 = jax.random.normal(ks[5], (MUL, MUL), dtype=jnp.float32)
        w_11_0 = jax.random.normal(ks[6], (MUL, MUL), dtype=jnp.float32)
        w_01_1 = jax.random.normal(ks[7], (MUL, MUL), dtype=jnp.float32)
        w_10_1 = jax.random.normal(ks[8], (MUL, MUL), dtype=jnp.float32)
        kf = jax.random.split(jax.random.fold_in(key, 1), 2)
        fc_w1 = jax.random.normal(kf[0], (10, 64), dtype=jnp.float32)
        fc_w2 = jax.random.normal(kf[1], (64, 1), dtype=jnp.float32)
        return {'node_in': node_in, 'edge_attr': edge_attr, 'edge_len_emb': edge_len_emb, 'w_00_0': w_00_0, 'w_11_0': w_11_0, 'w_01_1': w_01_1, 'w_10_1': w_10_1, 'fc_w1': fc_w1, 'fc_w2': fc_w2, 'edge_src': edge_src, 'edge_dst': edge_dst}
    _L0_gnn_all = _L0_gnn_setup()
    _L0_gnn_in = {k: v for k, v in _L0_gnn_all.items() if k in ('w_00_0', 'w_11_0', 'w_01_1', 'w_10_1', 'fc_w1', 'fc_w2')}
    del _L0_gnn_all

    def _L1_gnn_setup():
        import jax, jax.numpy as jnp
        import numpy as np
        N_NODES = 12500
        N_EDGES = 100000
        DIM = 256
        EPS = 1e-05
        key = jax.random.key(seed)
        ks = jax.random.split(key, 12)
        H = DIM
        s = 1.0 / np.sqrt(H)
        s2 = 1.0 / np.sqrt(2 * H)
        return {'feat': jax.random.normal(ks[0], (N_NODES, DIM), dtype=jnp.float32), 'src': jax.random.randint(ks[1], (N_EDGES,), 0, N_NODES, dtype=jnp.int32), 'dst': jax.random.randint(ks[2], (N_EDGES,), 0, N_NODES, dtype=jnp.int32), 'iw': jax.random.uniform(ks[3], (N_EDGES,), dtype=jnp.float32), 'ow': jax.random.uniform(ks[4], (N_EDGES,), dtype=jnp.float32), 'gamma': jnp.ones((DIM,), jnp.float32), 'beta': jnp.zeros((DIM,), jnp.float32), 'W_in': jax.random.uniform(ks[5], (H, H), jnp.float32, -s, s), 'b_in': jax.random.uniform(ks[6], (H,), jnp.float32, -s, s), 'W_out': jax.random.uniform(ks[7], (H, H), jnp.float32, -s, s), 'b_out': jax.random.uniform(ks[8], (H,), jnp.float32, -s, s), 'W_x2i': jax.random.uniform(ks[9], (2 * H, 2 * H), jnp.float32, -s2, s2), 'b_x2i': jax.random.uniform(ks[10], (2 * H,), jnp.float32, -s2, s2), 'W_h2h': jax.random.uniform(ks[11], (H, 2 * H), jnp.float32, -s, s)}
    _L1_gnn_all = _L1_gnn_setup()
    _L1_gnn_in = {k: v for k, v in _L1_gnn_all.items() if k in ('gamma', 'beta', 'W_in', 'b_in', 'W_out', 'b_out', 'W_x2i', 'b_x2i', 'W_h2h')}
    del _L1_gnn_all
    return {'x': x, 'src': src, 'dst': dst, 'edge_attr_10': edge_attr_10, 'edge_attr_4': edge_attr_4, 'edge_weight': edge_weight, 'edge_weight_n2': edge_weight_n2, 'L0_gnn_w_00_0': _L0_gnn_in['w_00_0'], 'L0_gnn_w_11_0': _L0_gnn_in['w_11_0'], 'L0_gnn_w_01_1': _L0_gnn_in['w_01_1'], 'L0_gnn_w_10_1': _L0_gnn_in['w_10_1'], 'L0_gnn_fc_w1': _L0_gnn_in['fc_w1'], 'L0_gnn_fc_w2': _L0_gnn_in['fc_w2'], 'L1_gnn_gamma': _L1_gnn_in['gamma'], 'L1_gnn_beta': _L1_gnn_in['beta'], 'L1_gnn_W_in': _L1_gnn_in['W_in'], 'L1_gnn_b_in': _L1_gnn_in['b_in'], 'L1_gnn_W_out': _L1_gnn_in['W_out'], 'L1_gnn_b_out': _L1_gnn_in['b_out'], 'L1_gnn_W_x2i': _L1_gnn_in['W_x2i'], 'L1_gnn_b_x2i': _L1_gnn_in['b_x2i'], 'L1_gnn_W_h2h': _L1_gnn_in['W_h2h']}

def reference(x, src, dst, edge_attr_10, edge_attr_4, edge_weight, edge_weight_n2, L0_gnn_w_00_0, L0_gnn_w_11_0, L0_gnn_w_01_1, L0_gnn_w_10_1, L0_gnn_fc_w1, L0_gnn_fc_w2, L1_gnn_gamma, L1_gnn_beta, L1_gnn_W_in, L1_gnn_b_in, L1_gnn_W_out, L1_gnn_b_out, L1_gnn_W_x2i, L1_gnn_b_x2i, L1_gnn_W_h2h):
    import jax
    import jax.numpy as jnp

    def _L0_gnn_ref(node_in, edge_attr, edge_len_emb, w_00_0, w_11_0, w_01_1, w_10_1, fc_w1, fc_w2, edge_src, edge_dst):
        import jax, jax.numpy as jnp
        import numpy as np
        MUL = 64
        N_NODES = 6250
        N_EDGES = 100000
        NUM_NEIGHBORS = 16.0
        SILU_NORM = 1.679177
        src = node_in[edge_src]
        s0 = src[:, :MUL]
        s1 = src[:, MUL:].reshape(-1, MUL, 3)
        a0 = edge_attr[:, 0:1]
        a1 = edge_attr[:, 1:4]
        alpha = np.float32(1.0 / np.sqrt(2.0 * MUL))
        inv_sqrt3 = np.float32(1.0 / np.sqrt(3.0))
        out0 = alpha * (jnp.einsum('ei,io->eo', s0 * a0, w_00_0) + inv_sqrt3 * jnp.einsum('eim,em,io->eo', s1, a1, w_11_0))
        out1 = alpha * (jnp.einsum('ei,io,em->eom', s0, w_01_1, a1) + jnp.einsum('eim,io->eom', s1 * a0[:, :, None], w_10_1))
        msg_ang = jnp.concatenate([out0, out1.reshape(-1, 3 * MUL)], axis=1)
        h = jax.nn.silu(edge_len_emb @ fc_w1 / np.float32(np.sqrt(10.0))) * np.float32(SILU_NORM)
        msg_rad = h @ fc_w2 / np.float32(np.sqrt(64.0))
        messages = msg_ang * msg_rad
        agg = jax.ops.segment_sum(messages, edge_dst, num_segments=node_in.shape[0])
        return agg / np.float32(np.sqrt(NUM_NEIGHBORS))

    def _L1_gnn_ref(feat, src, dst, iw, ow, gamma, beta, W_in, b_in, W_out, b_out, W_x2i, b_x2i, W_h2h):
        import jax, jax.numpy as jnp
        import numpy as np
        N_NODES = 12500
        N_EDGES = 100000
        DIM = 256
        EPS = 1e-05
        N = feat.shape[0]
        num_steps = 1
        mean = jnp.mean(feat, axis=0)
        var = jnp.var(feat, axis=0)
        h = (feat - mean) * jax.lax.rsqrt(var + EPS) * gamma + beta
        for _ in range(num_steps):
            feat_in = h @ W_in + b_in
            feat_out = h @ W_out + b_out
            a_in = jax.ops.segment_sum(feat_in[src] * iw[:, None], dst, num_segments=N)
            a_out = jax.ops.segment_sum(feat_out[dst] * ow[:, None], src, num_segments=N)
            a = jnp.concatenate((a_in, a_out), axis=1)
            xi = a @ W_x2i + b_x2i
            hh = h @ W_h2h
            i_i, i_n = jnp.split(xi, 2, axis=1)
            h_i, h_n = jnp.split(hh, 2, axis=1)
            input_gate = jax.nn.sigmoid(i_i + h_i)
            new_gate = jnp.tanh(i_n + h_n)
            h = new_gate + input_gate * (h - new_gate)
        return h
    x = _layernorm(x + _L0_gnn_ref(x, edge_attr_4, edge_attr_10, L0_gnn_w_00_0, L0_gnn_w_11_0, L0_gnn_w_01_1, L0_gnn_w_10_1, L0_gnn_fc_w1, L0_gnn_fc_w2, src, dst), axis=-1)
    x = _layernorm(x + _L1_gnn_ref(x, src, dst, edge_weight, edge_weight_n2, L1_gnn_gamma, L1_gnn_beta, L1_gnn_W_in, L1_gnn_b_in, L1_gnn_W_out, L1_gnn_b_out, L1_gnn_W_x2i, L1_gnn_b_x2i, L1_gnn_W_h2h), axis=-1)
    return x

_drawn_inputs = setup_inputs


def setup_inputs(seed=0):
    import zlib

    import numpy as np

    out = dict(_drawn_inputs(seed))
    spreads = {'L1_gnn_gamma': (1.0, 0.2), 'L1_gnn_beta': (0.0, 0.1)}
    factors = {'L1_gnn_b_x2i': 7.443}
    for name, (base, spread) in spreads.items():
        noise = np.random.default_rng([zlib.crc32(name.encode()), seed]).standard_normal(out[name].shape)
        drawn = base * np.exp(spread * noise) if base else spread * noise
        out[name] = jnp.asarray(drawn.astype(out[name].dtype))
    for name, factor in factors.items():
        out[name] = (out[name] * factor).astype(out[name].dtype)
    return out
```

```python
from contextlib import ExitStack

import concourse.bass as bass
from concourse import mybir

P = 128
N, E, D, MUL = 6250, 106250, 256, 64
NB = -(-N // P)
NP = NB * P
BG = 7
NG = NB // BG
T0 = 832
T = T0 + NB - 1
U = 4
R = 4
UT = U * R
FD, FS = 8, 4
DIN, SLOC, SW = 0, 1, 2
WIN = 6
ESUB = 1024
NSUB = T0 * P // 2 // ESUB
EPS = 1e-5
SILU_NORM = 1.679177
assert NB == BG * NG and T % UT == 0 and T0 % UT == 0 and NSUB % 2 == 0

ALU = mybir.AluOpType
ACT = mybir.ActivationFunctionType
F32 = mybir.dt.float32
I32 = mybir.dt.int32


class Chain:

    def __init__(self, eng, sem):
        self.eng, self.sem, self.n, self.i, self.per = eng, sem, 0, None, 0

    def loop(self, i, per):
        self.i, self.per, self.base = i, per, self.n

    def end(self, trips):
        assert self.n - self.base == self.per, (self.n - self.base, self.per)
        self.n = self.base + trips * self.per
        self.i = None

    def step(self, ins):
        ins.then_inc(self.sem, 1)
        self.n += 1

    def settle(self):
        self.eng.wait_ge(self.sem, self.n if self.i is None else self.i * self.per + self.n)

    def ordered(self, ins):
        self.step(ins)
        self.settle()


def build(nc, x, src_t, dst_t, attr_t, iw_t, ow_t, emb, w00, w11, w01, w10, fc1, fc2,
          gamma, beta, w_in, b_in, w_out, b_out, w_x2i, b_x2i, w_h2h, out):
    with ExitStack() as ctx:
        def sb(name, shape, dt=F32):
            return ctx.enter_context(nc.sbuf_tensor(name, shape, dt))

        def sem(name):
            return ctx.enter_context(nc.semaphore(name))

        rec_dst_dram = nc.dram_tensor("rec_dst", [P * T, FD], F32, kind="Internal").ap()
        rec_src_dram = nc.dram_tensor("rec_src", [P * T, FS], F32, kind="Internal").ap()
        feat_in_dram = nc.dram_tensor("feat_in", [NP, D], F32, kind="Internal").ap()
        feat_out_dram = nc.dram_tensor("feat_out", [NP, D], F32, kind="Internal").ap()
        x1_dram = nc.dram_tensor("x1", [NP, D], F32, kind="Internal").ap()
        h_dram = nc.dram_tensor("h", [NP, D], F32, kind="Internal").ap()

        acc = sb("acc", [P, NB * 2 * D])
        rows_buf = sb("rows_buf", [P, R * U, D])
        msg = sb("msg", [P, 2, U, 4, P])
        onehot = sb("onehot", [P, 2, U, P])
        prod = sb("prod", [P, U, MUL, 3])
        srt = sb("srt", [P, T + UT, FD])
        idx_stage = sb("idx_stage", [P, R, U], I32)
        stage_scatter = sb("stage_scatter", [P, R, U, FD])
        block_dst = sb("block_dst", [1, T + 2 * U], I32)
        block_src = sb("block_src", [1, T + 2 * U], I32)
        wx = sb("wx", [P, 6, 2 * D])
        wio = sb("wio", [P, 2, 2 * D])
        w_even = sb("w_even", [P, MUL])
        w_odd = sb("w_odd", [P, MUL])
        ident = sb("ident", [P, P])
        ones = sb("ones", [P, P])
        tri = sb("tri", [P, P])
        iota_row = sb("iota_row", [P, P])
        bias_io = sb("bias_io", [P, 2 * D])
        bias_x = sb("bias_x", [P, 2 * D])
        bn_a = sb("bn_a", [P, D])
        bn_b = sb("bn_b", [P, D])
        mean_row = sb("mean_row", [P, D])
        gates = sb("gates", [P, 2, 2 * D])
        stats = sb("stats", [P, BG, 6])
        mv = sb("mv", [P, BG, 2])
        rstd = sb("rstd", [P, BG])
        eps = sb("eps", [P, 1])
        small = sb("small", [P, 8, 64])
        fc1_bd = sb("fc1_bd", [20, P])
        fc2_bd = sb("fc2_bd", [P, 2])
        ps = [ctx.enter_context(nc.psum_tensor(f"ps{k}", [P, 512], F32)) for k in range(8)]

        at = [0]

        def part(words, dt=F32):
            v = acc[:, at[0]:at[0] + words]
            at[0] += words
            return v.bitcast(dt) if dt != F32 else v
        key_dst, key_src = part(T0, I32), part(T0, I32)
        attr = part(4 * T0).rearrange("p (t k) -> p t k", k=4)
        iw_sb, ow_sb = part(T0), part(T0)
        rec_dst = part(FD * T0).rearrange("p (t f) -> p t f", f=FD)
        rec_src = part(FS * T0).rearrange("p (t f) -> p t f", f=FS)
        rad = part(T0)
        blk_f, hot, scan, rank, tmp_f = (part(T0) for _ in range(5))
        tmp_i, addr_dst, addr_src = (part(T0, I32) for _ in range(3))
        assert at[0] <= NB * 2 * D
        emb_sb = rows_buf[0:20, 0:8, :].rearrange("p a b -> p (a b)").rearrange(
            "p (h e) -> p h e", h=2)
        hidden = msg[:, 0].rearrange("p u c f -> p (u c f)")[:, 0:1024].rearrange(
            "p (q e) -> p q e", q=2)
        iota_tile = msg[:, 1].rearrange("p u c f -> p (u c f)")[:, 0:T]
        past = msg[:, 1].rearrange("p u c f -> p (u c f)")[:, T:2 * T]
        zeros = rows_buf[:, 8:16, :].rearrange("p a b -> p (a b)")
        rows_flat = rows_buf[:, :, :].rearrange("p a b -> p (a b)")
        msg_flat = msg[:, :, :, :, :].rearrange("p a u c f -> p (a u c f)")
        stage = msg_flat[:, 0:BG * 2 * D].rearrange("p (b f) -> p b f", b=BG)
        stage_one = msg_flat[:, 0:BG * D].rearrange("p (b f) -> p b f", b=BG)
        stage_two = msg_flat[:, BG * D:2 * BG * D].rearrange("p (b f) -> p b f", b=BG)
        io_stage = rows_flat[:, 0:BG * 2 * D].rearrange("p (b f) -> p b f", b=BG)
        xin = rows_flat[:, 0:BG * D].rearrange("p (b f) -> p b f", b=BG)
        hin = rows_flat[:, BG * D:2 * BG * D].rearrange("p (b f) -> p b f", b=BG)
        bn_sd, bn_var = gates[:, 0, 0:D], gates[:, 0, D:2 * D]
        turned = [onehot[:, :, :, :].rearrange("p a u f -> p (a u f)")[:, 0:3 * D],
                  prod[:, :, :, :].rearrange("p u i m -> p (u i m)")[:, 0:3 * D]]

        s_in = {k: sem(f"s_in_{k}") for k in ("dst", "src", "attr", "weights", "rows")}
        s_emb = [sem(f"s_emb{h}") for h in range(2)]
        s_emb_free = sem("s_emb_free")
        s_hid_ps = sem("s_hid_ps")
        s_hid = sem("s_hid")
        s_rad_ps = sem("s_rad_ps")
        s_rad = sem("s_rad")
        s_const = sem("s_const")
        s_wconst = sem("s_wconst")
        s_cnt, s_cnt_ps = sem("s_cnt"), sem("s_cnt_ps")
        s_tend, s_tend_ps = sem("s_tend"), sem("s_tend_ps")
        s_past, s_past_ps = sem("s_past"), sem("s_past_ps")
        s_zero = sem("s_zero")
        s_zeroed = sem("s_zeroed")
        s_rec = sem("s_rec")
        s_scat = {k: [sem(f"s_scat_{k}{r}") for r in range(R)] for k in ("dst", "src")}
        s_dve, s_pool = sem("s_dve"), sem("s_pool")
        loops = {}
        for k in ("l0", "in", "out"):
            loops[k] = dict(
                srt=sem(f"s_srt_{k}"),
                idx=sem(f"s_idx_{k}"),
                got=[sem(f"s_got_{k}{r}") for r in range(R)],
                hot=sem(f"s_hot_{k}"),
                scaled=sem(f"s_scaled_{k}"),
                sums=sem(f"s_sums_{k}"),
                added=sem(f"s_added_{k}"),
            )
        s_srt_used = sem("s_srt_used")
        nodes = {name: {q: sem(f"s_node_{q}_{name}") for q in
                        ("staged", "turns", "copied", "sums", "used", "var", "sd")}
                 for name in ("l0", "io", "fin")}
        s_xin, s_x1 = sem("s_xin"), sem("s_x1")
        s_sum_ps, s_sq, s_sq_ps = sem("s_sum_ps"), sem("s_sq"), sem("s_sq_ps")
        s_bnv, s_bnsd = sem("s_bnv"), sem("s_bnsd")
        s_stored, s_io_dma = sem("s_stored"), sem("s_io_dma")
        s_fin_in, s_pre, s_mixed = sem("s_fin_in"), sem("s_pre"), sem("s_mixed")
        s_out, s_out_dma = sem("s_out"), sem("s_out_dma")

        def before(j):
            return 2 if j == 0 else 1

        s_pass = sem("s_pass")

        block = ctx.enter_context(nc.Block())

        def by_block(dram):
            return dram.rearrange("(b p) f -> p b f", p=P)

        def by_lane(dram, f):
            return dram.rearrange("(p t) f -> p t f", p=P)

        @block.sync
        def _(sp):
            sp.dma_start(key_dst, dst_t).then_inc(s_in["dst"], 16)
            sp.dma_start(key_src, src_t).then_inc(s_in["src"], 16)
            sp.dma_start(fc1_bd[0:10, 0:64], fc1).then_inc(s_in["weights"], 16)
            sp.dma_start(fc1_bd[10:20, 64:128], fc1).then_inc(s_in["weights"], 16)
            sp.dma_start(fc2_bd[0:64, 0:1], fc2).then_inc(s_in["weights"], 16)
            sp.dma_start(fc2_bd[64:128, 1:2], fc2).then_inc(s_in["weights"], 16)
            sp.wait_ge(s_zero, 1)
            sp.dma_start(fc1_bd[0:10, 64:128], zeros[0:10, 0:64]).then_inc(s_in["weights"], 16)
            sp.dma_start(fc1_bd[10:20, 0:64], zeros[0:10, 0:64]).then_inc(s_in["weights"], 16)
            sp.dma_start(fc2_bd[0:64, 1:2], zeros[0:64, 0:1]).then_inc(s_in["weights"], 16)
            sp.dma_start(fc2_bd[64:128, 0:1], zeros[0:64, 0:1]).then_inc(s_in["weights"], 16)
            flat = rec_dst_dram.rearrange("(p a t) f -> a p (t f)", p=P, a=4)
            for a in range(4):
                sp.dma_start(flat[a], zeros[:, 0:T // 4 * FD]).then_inc(s_zeroed, 16)
            flat = rec_src_dram.rearrange("(p a t) f -> a p (t f)", p=P, a=2)
            for a in range(2):
                sp.dma_start(flat[a], zeros[:, 0:T // 2 * FS]).then_inc(s_zeroed, 16)
            sp.dma_start(attr, attr_t).then_inc(s_in["attr"], 16)
            sp.dma_start(iw_sb, iw_t).then_inc(s_in["attr"], 16)
            sp.dma_start(ow_sb, ow_t).then_inc(s_in["attr"], 16)
            with sp.Fori(0, NSUB // 2) as i:
                for h in range(2):
                    sp.wait_ge(s_emb_free, 2 * i + h + 1)
                    sp.sem_inc(s_pass, 1)
                    sp.dma_start(emb_sb[:, h, :], emb[:, bass.ds((2 * i + h) * ESUB, ESUB)]
                                 ).then_inc(s_emb[h], 16)
            for k in range(4):
                sp.dma_start(wx[:, k, :], w_x2i[k * P:(k + 1) * P, :]).then_inc(s_in["rows"], 16)
            for k in range(2):
                sp.dma_start(wx[:, 4 + k, :], w_h2h[k * P:(k + 1) * P, :]).then_inc(s_in["rows"], 16)
                sp.dma_start(wio[:, k, 0:D], w_in[k * P:(k + 1) * P, :]).then_inc(s_in["rows"], 16)
                sp.dma_start(wio[:, k, D:2 * D], w_out[k * P:(k + 1) * P, :]).then_inc(s_in["rows"], 16)
            sp.dma_start(w_even[0:64, :], w00).then_inc(s_in["rows"], 16)
            sp.dma_start(w_even[64:128, :], w11).then_inc(s_in["rows"], 16)
            sp.dma_start(w_odd[0:64, :], w01).then_inc(s_in["rows"], 16)
            sp.dma_start(w_odd[64:128, :], w10).then_inc(s_in["rows"], 16)
            for to, of in ((bn_a[:], gamma), (bn_b[:], beta), (bias_io[:, 0:D], b_in),
                           (bias_io[:, D:2 * D], b_out), (bias_x[:], b_x2i)):
                sp.dma_start(to, of.to_broadcast([P, of.shape[1]])).then_inc(s_in["rows"], 16)

            for s in s_scat["dst"]:
                sp.wait_ge(s, 16 * U * (T0 // UT))
            sp.dma_start(srt[:, 0:T, :], by_lane(rec_dst_dram, FD)).then_inc(loops["l0"]["srt"], 16)

            sp.wait_ge(loops["l0"]["added"], 2 + T // U)
            with sp.Fori(0, NG) as i:
                sp.wait_ge(s_x1, i + 1)
                sp.sem_inc(s_pass, 1)
                sp.dma_start(xin, by_block(x)[:, bass.ds(BG * i, BG), :]).then_inc(s_xin, 16)

            acc_v = acc[:, :].rearrange("p (b f) -> p b f", b=NB)
            with sp.Fori(0, NG) as i:
                g = bass.ds(BG * i, BG)
                sp.wait_ge(nodes["io"]["staged"], i + 1)
                sp.sem_inc(s_pass, 1)
                sp.dma_start(by_block(x1_dram)[:, g, :], acc_v[:, g, 0:D]).then_inc(s_io_dma, 16)
                sp.dma_start(by_block(h_dram)[:, g, :], stage_one).then_inc(s_io_dma, 16)
                sp.wait_ge(nodes["io"]["used"], BG * i + BG + 2)
                sp.sem_inc(s_pass, 1)
                sp.dma_start(by_block(feat_in_dram)[:, g, :], io_stage[:, :, 0:D]).then_inc(s_io_dma, 16)
                sp.dma_start(by_block(feat_out_dram)[:, g, :], io_stage[:, :, D:2 * D]).then_inc(s_io_dma, 16)
                sp.wait_ge(s_io_dma, 64 * i + 64)
                sp.sem_inc(s_pass, 1)
                sp.sem_inc(s_stored, 1)

            for s in s_scat["src"]:
                sp.wait_ge(s, 16 * U * (T0 // UT))
            sp.wait_ge(s_srt_used, 1)
            srt_s = srt[:, :, :].rearrange("p t f -> p (t f)")[:, 0:T * FS]
            sp.dma_start(srt_s, rec_src_dram.rearrange("(p t) f -> p (t f)", p=P)
                         ).then_inc(loops["out"]["srt"], 16)

            sp.wait_ge(loops["out"]["sums"], R + T // U)
            out_full = out[0:(NB - 1) * P, :].rearrange("(b p) f -> p b f", p=P)

            def fetch(i):
                g = bass.ds(BG * i, BG)
                sp.dma_start(xin, by_block(x1_dram)[:, g, :]).then_inc(s_fin_in, 16)
                sp.dma_start(hin, by_block(h_dram)[:, g, :]).then_inc(s_fin_in, 16)
            with sp.Fori(0, NG - 1) as i:
                fetch(i)
                sp.wait_ge(s_out, i + 1)
                sp.sem_inc(s_pass, 1)
                sp.dma_start(out_full[:, bass.ds(BG * i, BG), :], xin).then_inc(s_out_dma, 16)
                sp.wait_ge(s_out_dma, 16 * i + 16)
                sp.sem_inc(s_pass, 1)
            fetch(NG - 1)
            sp.wait_ge(s_out, NG)
            sp.dma_start(out_full[:, BG * (NG - 1):NB - 1, :], xin[:, 0:BG - 1, :]).then_inc(s_out_dma, 16)
            rest = N - (NB - 1) * P
            sp.dma_start(out[(NB - 1) * P:N, :], xin[0:rest, BG - 1, :]).then_inc(s_out_dma, 16)
            sp.wait_ge(s_out_dma, 16 * (NG + 1))

        @block.gpsimd
        def _(pool):
            own = Chain(pool, s_pool)
            nc.gpsimd.memset(zeros, 0.0).then_inc(s_zero, 1)
            own.ordered(nc.gpsimd.memset(ones[:], 1.0))
            own.ordered(nc.gpsimd.memset(tri[:], 1.0))
            own.ordered(nc.gpsimd.memset(ident[:], 0.0))
            nc.gpsimd.memset(eps[:], EPS)
            own.ordered(nc.gpsimd.affine_select(out=tri[:], in_=tri[:], compare_op=ALU.is_gt, fill=0.0,
                                                base=0, pattern=[[1, P]], channel_multiplier=-1))
            own.ordered(nc.gpsimd.affine_select(out=ident[:], in_=ident[:], compare_op=ALU.not_equal,
                                                fill=1.0, base=0, pattern=[[1, P]], channel_multiplier=-1))
            nc.gpsimd.iota(iota_row[:], pattern=[[1, P]], base=0, channel_multiplier=0,
                           allow_small_or_imprecise_dtypes=True)
            own.ordered(nc.gpsimd.iota(iota_tile, pattern=[[1, T]], base=0, channel_multiplier=0,
                                       allow_small_or_imprecise_dtypes=True))
            pool.sem_inc(s_const, 1)

            def wait_here(s, v):
                pool.wait_ge(s, v)
                pool.sem_inc(s_pass, 1)

            pool.wait_ge(s_zeroed, 6 * 16)
            for n, (key, dram, f) in enumerate((("dst", rec_dst_dram, FD), ("src", rec_src_dram, FS))):
                with pool.Fori(0, T0 // UT) as i:
                    for r in range(R):
                        wait_here(s_rec, (n * (T0 // U) + R * i) + r + 1)
                        for u in range(U):
                            pool.indirect_dma_start(
                                out=dram, out_offset=bass.IndirectOffsetOnAxis(
                                    ap=idx_stage[:, r, u:u + 1], axis=0),
                                in_=stage_scatter[:, r, u, 0:f], in_offset=None,
                            ).then_inc(s_scat[key][r], 16)

            def gathers(k, table, free):
                with pool.Fori(0, T // UT) as i:
                    for r in range(R):
                        wait_here(k["idx"], R * i + r + 1)
                        for s in free:
                            wait_here(s, R * i + r + 1)
                        for u in range(U):
                            pool.indirect_dma_start(
                                out=rows_buf[:, U * r + u, :], out_offset=None, in_=table,
                                in_offset=bass.IndirectOffsetOnAxis(ap=idx_stage[:, r, u:u + 1], axis=0),
                            ).then_inc(k["got"][r], 16)

            k = loops["l0"]
            pool.sem_inc(k["hot"], R)
            pool.sem_inc(k["scaled"], R)
            gathers(k, x, (k["hot"], k["scaled"]))
            for name, table in (("in", feat_in_dram), ("out", feat_out_dram)):
                k = loops[name]
                pool.wait_ge(s_stored, NG + 1)
                gathers(k, table, (k["sums"],))

        @block.scalar
        def _(act):
            act.wait_ge(s_const, 1)
            rad_v = rad.rearrange("p (s t) -> p s t", s=2)
            with act.Fori(0, NSUB // 2) as i:
                for h in range(2):
                    act.wait_ge(s_hid_ps, 2 * i + h + 1)
                    for q in range(2):
                        ins = nc.scalar.activation(hidden[:, q, :], ps[q][:, :], ACT.Silu,
                                                   scale=1.0 / 10.0 ** 0.5)
                    ins.then_inc(s_hid, 1)
                    act.wait_ge(s_rad_ps, 2 * i + h + 1)
                    nc.scalar.copy(rad_v[:, :, bass.ds((2 * i + h) * (ESUB // P), ESUB // P)],
                                   ps[2][:, 0:2 * ESUB // P].rearrange("p (t s) -> p s t", s=2)
                                   ).then_inc(s_rad, 1)
            k = loops["l0"]
            act.wait_ge(k["srt"], 16)
            with act.Fori(0, T // UT) as i:
                for r in range(R):
                    act.wait_ge(k["got"][r], 16 * U * (i + 1))
                    act.wait_ge(k["sums"], R * i + r + 1)
                    for u in range(U):
                        row = rows_buf[:, U * r + u, :]
                        c0 = srt[:, bass.ds(UT * i + U * r + u, 1), SW:SW + 1].rearrange("p a b -> p (a b)")
                        nc.scalar.activation(msg[:, r % 2, u, 0, 0:MUL], row[:, 0:MUL], ACT.Copy, scale=c0)
                        ins = nc.scalar.activation(msg[:, r % 2, u, 1:4, MUL:P],
                                                   row[:, MUL:D].rearrange("p (i m) -> p m i", m=3),
                                                   ACT.Copy, scale=c0)
                    ins.then_inc(k["scaled"], 1)

            def copy_turned(st, i, j, width):
                act.wait_ge(st["turns"], BG * i + j + 1)
                act.wait_ge(st["sums"], BG * i + j + before(j))
                to = turned[j % 2]
                if width > 512:
                    nc.scalar.copy(to[:, 512:width], ps[2 + j % 2][:, 0:width - 512])
                nc.scalar.copy(to[:, 0:min(512, width)], ps[j % 2][:, 0:min(512, width)]
                               ).then_inc(st["copied"], 1)

            def deviations(st, i):
                act.wait_ge(st["var"], i + 1)
                nc.scalar.activation(rstd[:, :], mv[:, :, 1:2].rearrange("p b o -> p (b o)"), ACT.Sqrt,
                                     bias=eps[:, 0:1]).then_inc(st["sd"], 1)

            with act.Fori(0, NG) as i:
                for j in range(BG):
                    copy_turned(nodes["l0"], i, j, 512)
                deviations(nodes["l0"], i)
            act.wait_ge(s_bnv, 1)
            nc.scalar.activation(bn_sd, bn_var, ACT.Sqrt, bias=eps[:, 0:1]).then_inc(s_bnsd, 1)
            with act.Fori(0, NG) as i:
                for j in range(BG):
                    copy_turned(nodes["io"], i, j, 256)
            st = nodes["fin"]
            with act.Fori(0, NG) as i:
                for j in range(BG + 1):
                    if j < BG:
                        copy_turned(st, i, j, 768)
                    if j >= 1:
                        n = j - 1
                        act.wait_ge(s_pre, BG * i + n + 1)
                        act.wait_ge(s_mixed, BG * i + n + before(n))
                        nc.scalar.activation(gates[:, n % 2, 0:D], ps[4 + n % 2][:, 0:D], ACT.Sigmoid)
                        nc.scalar.activation(gates[:, n % 2, D:2 * D], ps[4 + n % 2][:, D:2 * D],
                                             ACT.Tanh).then_inc(st["used"], 1)
                deviations(st, i)

        @block.tensor
        def _(pe):
            pe.wait_ge(s_in["weights"], 8 * 16)
            pe.sem_inc(s_emb_free, 2)
            pe.sem_inc(s_rad, 1)
            with pe.Fori(0, NSUB // 2) as i:
                for h in range(2):
                    pe.wait_ge(s_emb[h], 16 * (i + 1))
                    pe.wait_ge(s_rad, 2 * i + h + 1)
                    for q in range(2):
                        ins = pe.matmul(ps[q][:, :], fc1_bd[:, :], emb_sb[:, h, 512 * q:512 * q + 512],
                                        start=True, stop=True)
                    ins.then_inc(s_hid_ps, 1)
                    pe.wait_ge(s_hid, 2 * i + h + 1)
                    for q in range(2):
                        for t in range(4):
                            c = 2 * (4 * q + t)
                            ins = pe.matmul(ps[2][:, c:c + 2], hidden[:, q, P * t:P * t + P], fc2_bd[:, :],
                                            start=True, stop=True)
                    ins.then_inc(s_rad_ps, 1)
                    pe.sem_inc(s_emb_free, 1)
            pe.wait_ge(s_const, 1)
            for n in range(2):
                pe.wait_ge(s_cnt, n + 1)
                pe.matmul(ps[3][:, 0:NB], tri[:, :], small[:, 0, 0:NB], start=True, stop=True)
                pe.matmul(ps[4][:, 0:NB], ones[:, :], small[:, 0, 0:NB], start=True, stop=True
                          ).then_inc(s_cnt_ps, 1)
                pe.wait_ge(s_tend, n + 1)
                pe.matmul(ps[3][0:NB, 0:1], small[0:1, 2, 0:NB], ones[0:1, 0:1], start=True, stop=True
                          ).then_inc(s_tend_ps, 1)
                pe.wait_ge(s_past, n + 1)
                pe.matmul(ps[3][:, 0:T // 2], ones[0:NB, :], past[0:NB, 0:T // 2], start=True, stop=True)
                pe.matmul(ps[4][:, 0:T // 2], ones[0:NB, :], past[0:NB, T // 2:T], start=True, stop=True
                          ).then_inc(s_past_ps, 1)

            def edge_sums(k, operands, rows, width):
                with pe.Fori(0, T // UT) as i:
                    for r in range(R):
                        for s, v in operands(i, r):
                            pe.wait_ge(s, v)
                        pe.wait_ge(k["added"], R * i + r + 1)
                        for u in range(U):
                            ins = pe.matmul(ps[U * (r % 2) + u][:, 0:width], onehot[:, r % 2, u, :],
                                            rows(r, u), start=True, stop=True)
                        ins.then_inc(k["sums"], 1)

            k0 = loops["l0"]
            edge_sums(k0, lambda i, r: ((k0["hot"], R * i + r + 1 + R), (k0["scaled"], R * i + r + 1 + R)),
                      lambda r, u: msg[:, r % 2, u, :, :].rearrange("p c f -> p (c f)"), 2 * D)

            def products(st, turn, product, ready):
                with pe.Fori(0, NG) as i:
                    for s, per in ready:
                        pe.wait_ge(s, per * (i + 1))
                    for j in range(BG + 1):
                        if j < BG:
                            pe.wait_ge(st["copied"], BG * i + j + before(j))
                            turn(j).then_inc(st["turns"], 1)
                        if j >= 1:
                            n = j - 1
                            pe.wait_ge(st["copied"], BG * i + n + 1 + 2)
                            pe.wait_ge(st["used"], BG * i + n + before(n))
                            product(n).then_inc(st["sums"], 1)

            def turn(parts, first_bank):
                for c, of in enumerate(parts):
                    ins = pe.transpose(ps[first_bank][:, P * c:P * c + P], of, ident[:, :])
                return ins

            def halves(v):
                return [v[:, 0:P], v[:, P:D]]

            def weights0(j):
                for c in range(4):
                    ins = pe.matmul(ps[4 + j % 2][:, MUL * c:MUL * c + MUL], turned[j % 2][:, P * c:P * c + P],
                                    (w_odd if c else w_even)[:, :], start=True, stop=True)
                return ins

            def weights(parts):
                def product(j):
                    for c, w in enumerate(parts):
                        ins = pe.matmul(ps[4 + j % 2][:, :], turned[j % 2][:, P * c:P * c + P], w,
                                        start=c == 0, stop=c == len(parts) - 1)
                    return ins
                return product

            pe.wait_ge(s_wconst, 1)
            products(nodes["l0"], lambda j: turn([stage[:, j, P * c:P * c + P] for c in range(4)], j % 2),
                     weights0, ((nodes["l0"]["staged"], 1),))

            acc_v = acc[:, :].rearrange("p (b f) -> p b f", b=NB)
            pe.wait_ge(s_x1, NG + 1)
            pe.matmul(ps[6][:, 0:D], ones[:, :], acc_v[:, 0, 0:D], start=True, stop=False)
            with pe.Fori(1, NB - 1) as b:
                pe.matmul(ps[6][:, 0:D], ones[:, :], acc_v[:, bass.ds(b, 1), 0:D].rearrange("p a f -> p (a f)"),
                          start=False, stop=False)
            pe.matmul(ps[6][:, 0:D], ones[:, :], acc_v[:, NB - 1, 0:D], start=False, stop=True
                      ).then_inc(s_sum_ps, 1)

            def squares(first, last):
                for j in range(BG):
                    ins = pe.matmul(ps[7][:, 0:D], ones[:, :], stage_one[:, j, :],
                                    start=first and j == 0, stop=last and j == BG - 1)
                ins.then_inc(s_sq_ps, 1)
            pe.wait_ge(s_sq, 1)
            squares(True, False)
            with pe.Fori(1, NG - 1) as i:
                pe.wait_ge(s_sq, i + 1)
                squares(False, False)
            pe.wait_ge(s_sq, NG)
            squares(False, True)

            products(nodes["io"], lambda j: turn(halves(stage_one[:, j, :]), j % 2),
                     weights([wio[:, 0, :], wio[:, 1, :]]), ((nodes["io"]["staged"], 1),))

            for name in ("in", "out"):
                k1 = loops[name]
                pe.sem_inc(k1["sums"], R)
                edge_sums(k1, lambda i, r: ((k1["hot"], R * i + r + 1), (k1["got"][r], 16 * U * (i + 1))),
                          lambda r, u: rows_buf[:, U * r + u, :], D)

            def turn_fin(j):
                turn(halves(hin[:, j, :]), 2 + j % 2)
                return turn(halves(stage_one[:, j, :]) + halves(stage_two[:, j, :]), j % 2)
            products(nodes["fin"], turn_fin, weights([wx[:, c, :] for c in range(6)]),
                     ((nodes["fin"]["staged"], 1), (s_fin_in, 32)))

        @block.vector
        def _(dve):
            own = Chain(dve, s_dve)
            V = nc.vector
            for k in loops.values():
                dve.sem_inc(k["added"], 2)
            for st in nodes.values():
                for name in ("copied", "sums", "used"):
                    dve.sem_inc(st[name], 2)
            dve.sem_inc(s_mixed, 2)
            dve.sem_inc(loops["l0"]["sums"], 2)
            own.step(V.memset(block_dst[:, :], 0))
            own.step(V.memset(block_src[:, :], 0))
            own.step(V.memset(srt[:, T:T + UT, :], 0.0))
            own.step(V.memset(stage_scatter[:, :, :, :], 0.0))
            own.step(V.memset(rec_dst[:, :, FD - 1:FD], 0.0))
            own.ordered(V.memset(rec_src[:, :, FS - 1:FS], 0.0))
            dve.wait_ge(s_const, 1)

            cnt, tend, tiles, tstart, base = (small[:, q, 0:NB] for q in (0, 2, 1, 3, 4))
            int_a, int_b = (small[:, q, 0:NB].bitcast(I32) for q in (5, 6))

            def positions(n, key, landed, rec, addr, table):
                dve.wait_ge(landed, 16)
                own.ordered(V.tensor_scalar(tmp_i, key, 7, None, ALU.arith_shift_right))
                own.ordered(V.tensor_copy(blk_f, tmp_i))
                own.ordered(V.tensor_scalar(tmp_i, key, 127, None, ALU.bitwise_and))
                own.step(V.tensor_copy(rec[:, :, SLOC], tmp_i))
                own.ordered(V.memset(rank, 0.0))
                with dve.Fori(0, NB) as b:
                    own.loop(b, 5)
                    own.ordered(V.tensor_scalar(hot, blk_f, iota_row[:, bass.ds(b, 1)], None, ALU.is_equal))
                    own.ordered(V.tensor_tensor_scan(scan, hot, hot, 0.0, ALU.add, ALU.max))
                    own.step(V.tensor_copy(small[:, 0, bass.ds(b, 1)], scan[:, T0 - 1:T0]))
                    own.ordered(V.tensor_tensor(tmp_f, hot, scan, ALU.mult))
                    own.ordered(V.tensor_tensor(rank, rank, tmp_f, ALU.add))
                    own.end(NB)
                dve.sem_inc(s_cnt, 1)
                dve.wait_ge(s_cnt_ps, n + 1)
                own.ordered(V.tensor_scalar(int_a, ps[4][:, 0:NB], float(P - 1), None, ALU.add))
                own.ordered(V.tensor_scalar(int_b, int_a, 7, None, ALU.arith_shift_right))
                own.ordered(V.tensor_copy(tiles, int_b))
                own.ordered(V.tensor_tensor_scan(tend, tiles, tiles, 0.0, ALU.add, ALU.max))
                own.ordered(V.tensor_tensor(tstart, tend, tiles, ALU.subtract))
                own.ordered(V.scalar_tensor_tensor(out=base, in0=tstart, scalar=float(P), in1=ps[3][:, 0:NB],
                                                   op0=ALU.mult, op1=ALU.add))
                own.ordered(V.tensor_scalar(base, base, -1.0, None, ALU.add))
                dve.sem_inc(s_tend, 1)
                dve.wait_ge(s_tend_ps, n + 1)
                own.ordered(V.tensor_copy(small[0:NB, 7, 0:1], ps[3][0:NB, 0:1]))
                own.ordered(V.tensor_scalar(past[0:NB, :], iota_tile[0:NB, :], small[0:NB, 7, 0:1], None, ALU.is_ge))
                dve.sem_inc(s_past, 1)
                dve.wait_ge(s_past_ps, n + 1)
                for q in range(2):
                    own.ordered(V.tensor_scalar(table[0:1, U + q * T // 2:U + (q + 1) * T // 2],
                                                ps[3 + q][0:1, 0:T // 2], float(NB - 1), None, ALU.min))
                with dve.Fori(0, NB) as b:
                    own.loop(b, 2)
                    own.ordered(V.tensor_scalar(tmp_f, blk_f, iota_row[:, bass.ds(b, 1)],
                                                small[:, 4, bass.ds(b, 1)], ALU.is_equal, ALU.mult))
                    own.ordered(V.tensor_tensor(rank, rank, tmp_f, ALU.add))
                    own.end(NB)
                own.ordered(V.tensor_copy(tmp_i, rank))
                own.ordered(V.tensor_scalar(addr, tmp_i, 7, None, ALU.arith_shift_right))
                own.ordered(V.tensor_copy(scan, addr))
                own.ordered(V.tensor_scalar(addr, tmp_i, 127, None, ALU.bitwise_and))
                own.ordered(V.tensor_copy(hot, addr))
                own.ordered(V.scalar_tensor_tensor(out=addr, in0=hot, scalar=float(T), in1=scan,
                                                   op0=ALU.mult, op1=ALU.add))

            positions(0, key_dst, s_in["dst"], rec_dst, addr_dst, block_dst)
            dve.wait_ge(s_in["src"], 16)
            dve.wait_ge(s_in["attr"], 48)
            dve.wait_ge(s_rad, 1 + NSUB)
            own.step(V.tensor_copy(rec_dst[:, :, DIN].bitcast(I32), key_src))
            own.step(V.tensor_copy(rec_src[:, :, DIN].bitcast(I32), key_dst))
            for c in range(4):
                own.step(V.scalar_tensor_tensor(out=rec_dst[:, :, SW + c], in0=attr[:, :, c],
                                                scalar=SILU_NORM / 8.0, in1=rad, op0=ALU.mult, op1=ALU.mult))
            own.step(V.tensor_copy(rec_dst[:, :, WIN], iw_sb))
            own.ordered(V.tensor_copy(rec_src[:, :, SW], ow_sb))

            def scatter_stage(key, rec, addr, f):
                def unit(i, r):
                    t = bass.ds(UT * i + U * r, U) if not isinstance(i, int) else slice(UT * i + U * r, UT * i + U * r + U)
                    V.tensor_copy(idx_stage[:, r, :], addr[:, t])
                    V.tensor_copy(stage_scatter[:, r, :, 0:f], rec[:, t, :]).then_inc(s_rec, 1)
                for r in range(R):
                    unit(0, r)
                with dve.Fori(1, T0 // UT) as i:
                    for r in range(R):
                        dve.wait_ge(s_scat[key][r], 16 * U * i)
                        unit(i, r)
            scatter_stage("dst", rec_dst, addr_dst, FD)
            positions(1, key_src, s_in["src"], rec_src, addr_src, block_src)
            for r in range(R):
                dve.wait_ge(s_scat["dst"][r], 16 * U * (T0 // UT))
            scatter_stage("src", rec_src, addr_src, FS)
            for r in range(R):
                dve.wait_ge(s_scat["src"][r], 16 * U * (T0 // UT))

            dve.wait_ge(s_in["rows"], 16 * 19)
            alpha = (2.0 * MUL) ** -0.5 / 4.0
            own.step(V.tensor_scalar(w_odd[:, :], w_odd[:, :], alpha, None, ALU.mult))
            own.step(V.tensor_scalar(w_even[0:64, :], w_even[0:64, :], alpha, None, ALU.mult))
            own.ordered(V.tensor_scalar(w_even[64:128, :], w_even[64:128, :], alpha * 3.0 ** -0.5, None, ALU.mult))
            dve.sem_inc(s_wconst, 1)

            def edge_loop(k, rec, table, width, offset, operands, per):
                if k is not loops["in"]:
                    dve.wait_ge(k["srt"], 16)
                index = rec[:, :, DIN].bitcast(I32)
                for r in range(R):
                    V.tensor_copy(idx_stage[:, r, :], index[:, U * r:U * r + U]).then_inc(k["idx"], 1)

                def add(first_place, half):
                    blocks = [dve.value_load(table[0:1, bass.ds(first_place + u, 1)], min_val=0, max_val=NB - 1)
                              for u in range(U)]
                    for u in range(U):
                        at = acc[:, bass.ds(blocks[u] * width + offset, width)]
                        own.ordered(V.tensor_tensor(at, at, ps[U * half + u][:, 0:width], ALU.add))

                for u in range(U):
                    V.memset(ps[U + u][:, 0:width], 0.0)
                own.ordered(V.memset(acc[:, offset:offset + NB * width], 0.0))
                with dve.Fori(0, T // UT) as i:
                    own.loop(i, R * (per + U))
                    for r in range(R):
                        dve.wait_ge(k["got"][r], 16 * U * (i + 1))
                        V.tensor_copy(idx_stage[:, r, :], index[:, bass.ds(UT * i + UT + U * r, U)]
                                      ).then_inc(k["idx"], 1)
                        operands(i, r)
                        if r == 0:
                            dve.wait_ge(k["sums"], R * i + credit_sums[width])
                        else:
                            dve.wait_ge(k["sums"], R * i + r + credit_sums[width])
                        add(UT * i + U * r, (r + 1) % 2)
                        dve.sem_inc(k["added"], 1)
                    own.end(T // UT)
                dve.wait_ge(k["sums"], T // U + credit_sums[width])
                add(T, 1)

            credit_sums = {2 * D: 2, D: R}

            def operands0(i, r):
                k, h = loops["l0"], r % 2
                t = bass.ds(UT * i + U * r, U)
                g = rows_buf[:, U * r:U * r + U, :]
                s1 = g[:, :, MUL:D].rearrange("p u (i m) -> p u i m", m=3)
                cm = srt[:, t, SW + 1:SW + 4]
                dve.wait_ge(k["sums"], R * i + r + 1)
                own.step(V.tensor_tensor(onehot[:, h, :, :], srt[:, t, SLOC:SLOC + 1].to_broadcast([P, U, P]),
                                         iota_row[:, :].unsqueeze(1).to_broadcast([P, U, P]), ALU.is_equal))
                own.step(V.tensor_tensor(msg[:, h, :, 1:4, 0:MUL],
                                         g[:, :, 0:MUL].unsqueeze(2).to_broadcast([P, U, 3, MUL]),
                                         cm.unsqueeze(3).to_broadcast([P, U, 3, MUL]), ALU.mult))
                own.ordered(V.tensor_tensor(prod[:, :, :, :], s1,
                                            cm.unsqueeze(2).to_broadcast([P, U, MUL, 3]), ALU.mult))
                own.ordered(V.tensor_reduce(msg[:, h, :, 0, MUL:P], prod[:, :, :, :], mybir.AxisListType.X, ALU.add))
                dve.sem_inc(k["hot"], 1)

            edge_loop(loops["l0"], srt, block_dst, 2 * D, 0, operands0, 4)

            acc_v = acc[:, :].rearrange("p (b f) -> p b f", b=NB)
            dve.sem_inc(s_x1, 1)

            def normalise(st, i, to):
                for j in range(BG):
                    own.step(V.bn_stats(stats[:, j, :], to[:, j, :]))
                own.settle()
                dve.sem_inc(s_pass, 1)
                for j in range(BG):
                    own.step(V.bn_aggr(mv[:, j, :], stats[:, j, :]))
                own.settle()
                dve.sem_inc(st["var"], 1)
                dve.wait_ge(st["sd"], i + 1)
                own.ordered(V.reciprocal(rstd[:, :], rstd[:, :]))

            st = nodes["l0"]
            with dve.Fori(0, NG) as i:
                own.loop(i, 1 + 2 * BG + 2 * BG + 1 + BG)
                group = bass.ds(BG * i, BG)
                own.ordered(V.tensor_copy(stage, acc_v[:, group, :]))
                dve.sem_inc(st["staged"], 1)
                dve.wait_ge(s_xin, 16 * (i + 1))
                for j in range(BG):
                    dve.wait_ge(st["sums"], BG * i + j + 1 + 2)
                    y = ps[4 + j % 2]
                    own.step(V.tensor_tensor(xin[:, j, 0:MUL], xin[:, j, 0:MUL], y[:, 0:MUL], ALU.add))
                    v = xin[:, j, MUL:D].rearrange("p (o m) -> p m o", m=3)
                    own.ordered(V.tensor_tensor(v, v, y[:, MUL:D].rearrange("p (m o) -> p m o", m=3), ALU.add))
                    dve.sem_inc(st["used"], 1)
                normalise(st, i, xin)
                for j in range(BG):
                    own.step(V.tensor_scalar(acc_v[:, bass.ds(BG * i + j, 1), 0:D].rearrange("p a f -> p (a f)"),
                                             xin[:, j, :], mv[:, j, 0:1], rstd[:, j:j + 1], ALU.subtract, ALU.mult))
                own.settle()
                dve.sem_inc(s_x1, 1)
                own.end(NG)

            dve.wait_ge(s_sum_ps, 1)
            own.ordered(V.tensor_scalar(mean_row[:, :], ps[6][:, 0:D], 1.0 / N, None, ALU.mult))

            def squares(i):
                x1 = acc_v[:, bass.ds(BG * i, BG), 0:D] if not isinstance(i, int) else acc_v[:, 0:BG, 0:D]
                own.ordered(V.tensor_tensor(stage_one, x1, mean_row[:, :].unsqueeze(1).to_broadcast([P, BG, D]),
                                            ALU.subtract))
                own.ordered(V.tensor_tensor(stage_one, stage_one, stage_one, ALU.mult))
                dve.sem_inc(s_sq, 1)
            squares(0)
            with dve.Fori(1, NG) as i:
                dve.wait_ge(s_sq_ps, i)
                own.loop(i - 1, 2)
                squares(i)
                own.end(NG - 1)
            dve.wait_ge(s_sq_ps, NG)
            own.ordered(V.tensor_tensor(bn_sd, mean_row[:, :], mean_row[:, :], ALU.mult))
            own.ordered(V.scalar_tensor_tensor(out=bn_var, in0=bn_sd, scalar=-float(NP - N), in1=ps[7][:, 0:D],
                                               op0=ALU.mult, op1=ALU.add))
            own.ordered(V.tensor_scalar(bn_var, bn_var, 1.0 / N, None, ALU.mult))
            dve.sem_inc(s_bnv, 1)
            dve.wait_ge(s_bnsd, 1)
            own.ordered(V.reciprocal(bn_sd, bn_sd))
            own.ordered(V.tensor_tensor(bn_a[:, :], bn_a[:, :], bn_sd, ALU.mult))
            own.ordered(V.tensor_tensor(bn_sd, mean_row[:, :], bn_a[:, :], ALU.mult))
            own.ordered(V.tensor_tensor(bn_b[:, :], bn_b[:, :], bn_sd, ALU.subtract))

            st = nodes["io"]
            dve.sem_inc(s_stored, 1)
            with dve.Fori(0, NG) as i:
                own.loop(i, 2 + BG)
                x1 = acc_v[:, bass.ds(BG * i, BG), 0:D]
                dve.wait_ge(s_stored, i + 1)
                own.ordered(V.tensor_tensor(stage_one, x1, bn_a[:, :].unsqueeze(1).to_broadcast([P, BG, D]), ALU.mult))
                own.ordered(V.tensor_tensor(stage_one, stage_one, bn_b[:, :].unsqueeze(1).to_broadcast([P, BG, D]),
                                            ALU.add))
                dve.sem_inc(st["staged"], 1)
                for j in range(BG):
                    dve.wait_ge(st["sums"], BG * i + j + 1 + 2)
                    own.ordered(V.tensor_tensor(io_stage[:, j, :], ps[4 + j % 2][:, :], bias_io[:, :], ALU.add))
                    dve.sem_inc(st["used"], 1)
                own.end(NG)
            dve.wait_ge(s_stored, NG + 1)

            def operands1(k, rec, w):
                def operands(i, r):
                    dve.wait_ge(k["sums"], R * i + r + 1 + R - 2)
                    for u in range(U):
                        t = bass.ds(UT * i + U * r + u, 1)
                        own.step(V.tensor_scalar(onehot[:, r % 2, u, :], iota_row[:, :], rec[:, t, SLOC],
                                                 rec[:, t, w], ALU.is_equal, ALU.mult))
                    own.settle()
                    dve.sem_inc(k["hot"], 1)
                return operands
            edge_loop(loops["in"], srt, block_dst, D, 0, operands1(loops["in"], srt, WIN), U)
            dve.sem_inc(s_srt_used, 1)
            srt_s = srt[:, :, :].rearrange("p t f -> p (t f)")[:, 0:(T + UT) * FS].rearrange("p (t f) -> p t f", f=FS)
            own.ordered(V.memset(srt_s[:, T:T + UT, :], 0.0))
            edge_loop(loops["out"], srt_s, block_src, D, NB * D, operands1(loops["out"], srt_s, SW), U)

            st = nodes["fin"]
            a_in = acc[:, 0:NB * D].rearrange("p (b f) -> p b f", b=NB)
            a_out = acc[:, NB * D:2 * NB * D].rearrange("p (b f) -> p b f", b=NB)
            with dve.Fori(0, NG) as i:
                own.loop(i, 2 + 5 * BG + 2 * BG + 1 + BG)
                group = bass.ds(BG * i, BG)
                own.step(V.tensor_copy(stage_one, a_in[:, group, :]))
                own.ordered(V.tensor_copy(stage_two, a_out[:, group, :]))
                dve.sem_inc(st["staged"], 1)
                dve.wait_ge(s_fin_in, 32 * (i + 1))
                for j in range(BG + 1):
                    if j < BG:
                        y = ps[4 + j % 2]
                        dve.wait_ge(st["sums"], BG * i + j + 1 + 2)
                        own.ordered(V.tensor_tensor(y[:, :], y[:, :], bias_x[:, :], ALU.add))
                        dve.sem_inc(s_pre, 1)
                    if j >= 1:
                        n = j - 1
                        gate, new = gates[:, n % 2, 0:D], gates[:, n % 2, D:2 * D]
                        dve.wait_ge(st["used"], BG * i + n + 1 + 2)
                        own.ordered(V.tensor_tensor(hin[:, n, :], hin[:, n, :], new, ALU.subtract))
                        own.step(V.tensor_tensor(xin[:, n, :], xin[:, n, :], new, ALU.add))
                        own.ordered(V.tensor_tensor(hin[:, n, :], hin[:, n, :], gate, ALU.mult))
                        own.ordered(V.tensor_tensor(xin[:, n, :], xin[:, n, :], hin[:, n, :], ALU.add))
                        dve.sem_inc(s_mixed, 1)
                normalise(st, i, xin)
                for j in range(BG):
                    own.step(V.tensor_scalar(xin[:, j, :], xin[:, j, :], mv[:, j, 0:1], rstd[:, j:j + 1],
                                             ALU.subtract, ALU.mult))
                own.settle()
                dve.sem_inc(s_out, 1)
                own.end(NG)


def kernel(x, src, dst, edge_attr_10, edge_attr_4, edge_weight, edge_weight_n2,
           L0_gnn_w_00_0, L0_gnn_w_11_0, L0_gnn_w_01_1, L0_gnn_w_10_1, L0_gnn_fc_w1, L0_gnn_fc_w2,
           L1_gnn_gamma, L1_gnn_beta, L1_gnn_W_in, L1_gnn_b_in, L1_gnn_W_out, L1_gnn_b_out,
           L1_gnn_W_x2i, L1_gnn_b_x2i, L1_gnn_W_h2h):
    import numpy as np
    import concourse.bacc as bacc
    from concourse.bass_utils import run_bass_kernel_spmd

    EP = T0 * P

    def by_tile(a, fill=0):
        a = np.asarray(a)
        whole = np.full((EP,) + a.shape[1:], fill, a.dtype)
        whole[:E] = a
        whole = whole.reshape((T0, P) + a.shape[1:]).swapaxes(0, 1)
        return np.ascontiguousarray(whole.reshape(P, -1))

    emb = np.zeros((EP, 10), np.float32)
    emb[:E] = np.asarray(edge_attr_10)
    x_pad = np.zeros((NP, D), np.float32)
    x_pad[:N] = np.asarray(x)
    arrays = {
        "x": x_pad,
        "src_t": by_tile(src, N - 1), "dst_t": by_tile(dst, N - 1),
        "attr_t": by_tile(edge_attr_4), "iw_t": by_tile(edge_weight), "ow_t": by_tile(edge_weight_n2),
        "emb": np.ascontiguousarray(emb.reshape(2, EP // 2, 10).transpose(0, 2, 1).reshape(20, EP // 2)),
        "w00": L0_gnn_w_00_0, "w11": L0_gnn_w_11_0, "w01": L0_gnn_w_01_1, "w10": L0_gnn_w_10_1,
        "fc1": L0_gnn_fc_w1, "fc2": L0_gnn_fc_w2,
        "gamma": np.asarray(L1_gnn_gamma)[None], "beta": np.asarray(L1_gnn_beta)[None],
        "w_in": L1_gnn_W_in, "b_in": np.asarray(L1_gnn_b_in)[None],
        "w_out": L1_gnn_W_out, "b_out": np.asarray(L1_gnn_b_out)[None],
        "w_x2i": L1_gnn_W_x2i, "b_x2i": np.asarray(L1_gnn_b_x2i)[None], "w_h2h": L1_gnn_W_h2h,
    }
    nc = bacc.Bacc("TRN2", target_bir_lowering=False, num_devices=1)
    args, ins = [], {}
    for name, a in arrays.items():
        a = np.ascontiguousarray(np.asarray(a))
        ins["in_" + name] = a
        args.append(nc.dram_tensor("in_" + name, list(a.shape), mybir.dt.from_np(a.dtype),
                                   kind="ExternalInput").ap())
    result = nc.dram_tensor("out_0", [N, D], F32, kind="ExternalOutput").ap()
    build(nc, *args, result)
    r = run_bass_kernel_spmd(nc, [ins], core_ids=[0])
    return r.results[0]["out_0"]
```

```python
from contextlib import ExitStack

import concourse.bass as bass
from concourse import mybir

P = 128
N, E, D, MUL = 6250, 106250, 256, 64
NB = -(-N // P)
NP = NB * P
BG = 7
NG = NB // BG
T0 = 832
PAIRS = T0 // 2 + NB - 1
T = 2 * PAIRS
PAIR_BITS = 8
U = 4
R = 4
UT = U * R
LAG = U
FD, FS = 8, 4
DIN, SLOC, SW = 0, 1, 2
WIN = 6
ESUB = 1024
NSUB = T0 * P // 2 // ESUB
EPS = 1e-5
SILU_NORM = 1.679177
assert NB == BG * NG and T % UT == 0 and T0 % UT == 0 and NSUB % 2 == 0

ALU = mybir.AluOpType
ACT = mybir.ActivationFunctionType
F32 = mybir.dt.float32
I32 = mybir.dt.int32


class Chain:

    def __init__(self, eng, sem):
        self.eng, self.sem, self.n, self.i, self.per = eng, sem, 0, None, 0

    def loop(self, i, per):
        self.i, self.per, self.base = i, per, self.n

    def end(self, trips):
        assert self.n - self.base == self.per, (self.n - self.base, self.per)
        self.n = self.base + trips * self.per
        self.i = None

    def step(self, ins):
        ins.then_inc(self.sem, 1)
        self.n += 1

    def settle(self):
        self.eng.wait_ge(self.sem, self.n if self.i is None else self.i * self.per + self.n)

    def ordered(self, ins):
        self.step(ins)
        self.settle()


def build(nc, x, src_t, dst_t, attr_t, iw_t, ow_t, emb, w00, w11, w01, w10, fc1, fc2,
          gamma, beta, w_in, b_in, w_out, b_out, w_x2i, b_x2i, w_h2h, out):
    with ExitStack() as ctx:
        def sb(name, shape, dt=F32):
            return ctx.enter_context(nc.sbuf_tensor(name, shape, dt))

        def sem(name):
            return ctx.enter_context(nc.semaphore(name))

        rec_dst_dram = nc.dram_tensor("rec_dst", [P * T, FD], F32, kind="Internal").ap()
        rec_src_dram = nc.dram_tensor("rec_src", [P * T, FS], F32, kind="Internal").ap()
        feat_in_dram = nc.dram_tensor("feat_in", [NP, D], F32, kind="Internal").ap()
        feat_out_dram = nc.dram_tensor("feat_out", [NP, D], F32, kind="Internal").ap()
        x1_dram = nc.dram_tensor("x1", [NP, D], F32, kind="Internal").ap()
        h_dram = nc.dram_tensor("h", [NP, D], F32, kind="Internal").ap()

        acc = sb("acc", [P, NB * 2 * D])
        rows_buf = sb("rows_buf", [P, R * U, D])
        msg = sb("msg", [P, 2, 2, U, D])
        onehot = sb("onehot", [P, 2, U, P])
        onehot_c0 = sb("onehot_c0", [P, 2, U, P])
        prod = sb("prod", [P, U, MUL, 3])
        srt = sb("srt", [P, T + UT, FD])
        idx_stage = sb("idx_stage", [P, R, U], I32)
        stage_scatter = sb("stage_scatter", [P, R, U, FD])
        block_dst = sb("block_dst", [1, LAG + PAIRS + LAG], I32)
        block_src = sb("block_src", [1, LAG + PAIRS + LAG], I32)
        wx = sb("wx", [P, 6, 2 * D])
        wio = sb("wio", [P, 2, 2 * D])
        w_even = sb("w_even", [P, MUL])
        w_odd = sb("w_odd", [P, MUL])
        ident = sb("ident", [P, P])
        ones = sb("ones", [P, P])
        tri = sb("tri", [P, P])
        iota_row = sb("iota_row", [P, P])
        bias_io = sb("bias_io", [P, 2 * D])
        bias_x = sb("bias_x", [P, 2 * D])
        bn_a = sb("bn_a", [P, D])
        bn_b = sb("bn_b", [P, D])
        mean_row = sb("mean_row", [P, D])
        gates = sb("gates", [P, 2, 2 * D])
        stats = sb("stats", [P, BG, 6])
        mv = sb("mv", [P, BG, 2])
        rstd = sb("rstd", [P, BG])
        eps = sb("eps", [P, 1])
        small = sb("small", [P, 8, 64])
        fc1_bd = sb("fc1_bd", [20, P])
        fc2_bd = sb("fc2_bd", [P, 2])
        ps = [ctx.enter_context(nc.psum_tensor(f"ps{k}", [P, 512], F32)) for k in range(8)]

        at = [0]

        def part(words, dt=F32):
            v = acc[:, at[0]:at[0] + words]
            at[0] += words
            return v.bitcast(dt) if dt != F32 else v
        key_dst, key_src = part(T0, I32), part(T0, I32)
        attr = part(4 * T0).rearrange("p (t k) -> p t k", k=4)
        iw_sb, ow_sb = part(T0), part(T0)
        rec_dst = part(FD * T0).rearrange("p (t f) -> p t f", f=FD)
        rec_src = part(FS * T0).rearrange("p (t f) -> p t f", f=FS)
        rad = part(T0)
        blk_f, hot, scan, rank, tmp_f = (part(T0) for _ in range(5))
        tmp_i, addr_dst, addr_src = (part(T0, I32) for _ in range(3))
        assert at[0] <= NB * 2 * D
        emb_sb = rows_buf[0:20, 0:8, :].rearrange("p a b -> p (a b)").rearrange(
            "p (h e) -> p h e", h=2)
        hidden = msg[:, 0].rearrange("p a u f -> p (a u f)")[:, 0:1024].rearrange(
            "p (q e) -> p q e", q=2)
        iota_pair = msg[:, 1].rearrange("p a u f -> p (a u f)")[:, 0:PAIRS]
        past = msg[:, 1].rearrange("p a u f -> p (a u f)")[:, PAIRS:2 * PAIRS]
        zeros = rows_buf[:, 8:16, :].rearrange("p a b -> p (a b)")
        rows_flat = rows_buf[:, :, :].rearrange("p a b -> p (a b)")
        msg_flat = msg[:, :, :, :, :].rearrange("p a b u f -> p (a b u f)")
        stage = msg_flat[:, 0:BG * 2 * D].rearrange("p (b f) -> p b f", b=BG)
        stage_one = msg_flat[:, 0:BG * D].rearrange("p (b f) -> p b f", b=BG)
        stage_two = msg_flat[:, BG * D:2 * BG * D].rearrange("p (b f) -> p b f", b=BG)
        io_stage = rows_flat[:, 0:BG * 2 * D].rearrange("p (b f) -> p b f", b=BG)
        xin = rows_flat[:, 0:BG * D].rearrange("p (b f) -> p b f", b=BG)
        hin = rows_flat[:, BG * D:2 * BG * D].rearrange("p (b f) -> p b f", b=BG)
        bn_sd, bn_var = gates[:, 0, 0:D], gates[:, 0, D:2 * D]
        turned = [onehot[:, :, :, :].rearrange("p a u f -> p (a u f)")[:, 0:3 * D],
                  prod[:, :, :, :].rearrange("p u i m -> p (u i m)")[:, 0:3 * D]]

        s_in = {k: sem(f"s_in_{k}") for k in ("dst", "src", "attr", "weights", "rows")}
        s_emb = [sem(f"s_emb{h}") for h in range(2)]
        s_emb_free = sem("s_emb_free")
        s_hid_ps = sem("s_hid_ps")
        s_hid = sem("s_hid")
        s_rad_ps = sem("s_rad_ps")
        s_rad = sem("s_rad")
        s_const = sem("s_const")
        s_wconst = sem("s_wconst")
        s_cnt, s_cnt_ps = sem("s_cnt"), sem("s_cnt_ps")
        s_tend, s_tend_ps = sem("s_tend"), sem("s_tend_ps")
        s_past, s_past_ps = sem("s_past"), sem("s_past_ps")
        s_zero = sem("s_zero")
        s_zeroed = sem("s_zeroed")
        s_rec = sem("s_rec")
        s_scat = {k: [sem(f"s_scat_{k}{r}") for r in range(R)] for k in ("dst", "src")}
        s_dve, s_pool = sem("s_dve"), sem("s_pool")
        loops = {}
        for k in ("l0", "in", "out"):
            loops[k] = dict(
                srt=sem(f"s_srt_{k}"),
                idx=sem(f"s_idx_{k}"),
                got=[sem(f"s_got_{k}{r}") for r in range(R)],
                hot=sem(f"s_hot_{k}"),
                scaled=sem(f"s_scaled_{k}"),
                sums=sem(f"s_sums_{k}"),
                added=sem(f"s_added_{k}"),
            )
        s_flags = sem("s_flags")
        s_srt_used = sem("s_srt_used")
        nodes = {name: {q: sem(f"s_node_{q}_{name}") for q in
                        ("staged", "turns", "copied", "sums", "used", "var", "sd")}
                 for name in ("l0", "io", "fin")}
        s_xin, s_x1 = sem("s_xin"), sem("s_x1")
        s_sum_ps, s_sq, s_sq_ps = sem("s_sum_ps"), sem("s_sq"), sem("s_sq_ps")
        s_bnv, s_bnsd = sem("s_bnv"), sem("s_bnsd")
        s_stored, s_io_dma = sem("s_stored"), sem("s_io_dma")
        s_fin_in, s_pre, s_mixed = sem("s_fin_in"), sem("s_pre"), sem("s_mixed")
        s_out, s_out_dma = sem("s_out"), sem("s_out_dma")

        def before(j):
            return 2 if j == 0 else 1

        s_pass = sem("s_pass")

        block = ctx.enter_context(nc.Block())

        def by_block(dram):
            return dram.rearrange("(b p) f -> p b f", p=P)

        def by_lane(dram, f):
            return dram.rearrange("(p t) f -> p t f", p=P)

        @block.sync
        def _(sp):
            sp.dma_start(key_dst, dst_t).then_inc(s_in["dst"], 16)
            sp.dma_start(key_src, src_t).then_inc(s_in["src"], 16)
            sp.dma_start(fc1_bd[0:10, 0:64], fc1).then_inc(s_in["weights"], 16)
            sp.dma_start(fc1_bd[10:20, 64:128], fc1).then_inc(s_in["weights"], 16)
            sp.dma_start(fc2_bd[0:64, 0:1], fc2).then_inc(s_in["weights"], 16)
            sp.dma_start(fc2_bd[64:128, 1:2], fc2).then_inc(s_in["weights"], 16)
            sp.wait_ge(s_zero, 1)
            sp.dma_start(fc1_bd[0:10, 64:128], zeros[0:10, 0:64]).then_inc(s_in["weights"], 16)
            sp.dma_start(fc1_bd[10:20, 0:64], zeros[0:10, 0:64]).then_inc(s_in["weights"], 16)
            sp.dma_start(fc2_bd[0:64, 1:2], zeros[0:64, 0:1]).then_inc(s_in["weights"], 16)
            sp.dma_start(fc2_bd[64:128, 0:1], zeros[0:64, 0:1]).then_inc(s_in["weights"], 16)
            flat = rec_dst_dram.rearrange("(p a t) f -> a p (t f)", p=P, a=4)
            for a in range(4):
                sp.dma_start(flat[a], zeros[:, 0:T // 4 * FD]).then_inc(s_zeroed, 16)
            flat = rec_src_dram.rearrange("(p a t) f -> a p (t f)", p=P, a=2)
            for a in range(2):
                sp.dma_start(flat[a], zeros[:, 0:T // 2 * FS]).then_inc(s_zeroed, 16)
            sp.dma_start(attr, attr_t).then_inc(s_in["attr"], 16)
            sp.dma_start(iw_sb, iw_t).then_inc(s_in["attr"], 16)
            sp.dma_start(ow_sb, ow_t).then_inc(s_in["attr"], 16)
            with sp.Fori(0, NSUB // 2) as i:
                for h in range(2):
                    sp.wait_ge(s_emb_free, 2 * i + h + 1)
                    sp.sem_inc(s_pass, 1)
                    sp.dma_start(emb_sb[:, h, :], emb[:, bass.ds((2 * i + h) * ESUB, ESUB)]
                                 ).then_inc(s_emb[h], 16)
            for k in range(4):
                sp.dma_start(wx[:, k, :], w_x2i[k * P:(k + 1) * P, :]).then_inc(s_in["rows"], 16)
            for k in range(2):
                sp.dma_start(wx[:, 4 + k, :], w_h2h[k * P:(k + 1) * P, :]).then_inc(s_in["rows"], 16)
                sp.dma_start(wio[:, k, 0:D], w_in[k * P:(k + 1) * P, :]).then_inc(s_in["rows"], 16)
                sp.dma_start(wio[:, k, D:2 * D], w_out[k * P:(k + 1) * P, :]).then_inc(s_in["rows"], 16)
            sp.dma_start(w_even[0:64, :], w00).then_inc(s_in["rows"], 16)
            sp.dma_start(w_even[64:128, :], w11).then_inc(s_in["rows"], 16)
            sp.dma_start(w_odd[0:64, :], w01).then_inc(s_in["rows"], 16)
            sp.dma_start(w_odd[64:128, :], w10).then_inc(s_in["rows"], 16)
            for to, of in ((bn_a[:], gamma), (bn_b[:], beta), (bias_io[:, 0:D], b_in),
                           (bias_io[:, D:2 * D], b_out), (bias_x[:], b_x2i)):
                sp.dma_start(to, of.to_broadcast([P, of.shape[1]])).then_inc(s_in["rows"], 16)

            for s in s_scat["dst"]:
                sp.wait_ge(s, 16 * U * (T0 // UT))
            sp.dma_start(srt[:, 0:T, :], by_lane(rec_dst_dram, FD)).then_inc(loops["l0"]["srt"], 16)

            sp.wait_ge(loops["l0"]["sums"], R + T // U)
            with sp.Fori(0, NG) as i:
                sp.wait_ge(s_x1, i + 1)
                sp.sem_inc(s_pass, 1)
                sp.dma_start(xin, by_block(x)[:, bass.ds(BG * i, BG), :]).then_inc(s_xin, 16)

            acc_v = acc[:, :].rearrange("p (b f) -> p b f", b=NB)
            with sp.Fori(0, NG) as i:
                g = bass.ds(BG * i, BG)
                sp.wait_ge(nodes["io"]["staged"], i + 1)
                sp.sem_inc(s_pass, 1)
                sp.dma_start(by_block(x1_dram)[:, g, :], acc_v[:, g, 0:D]).then_inc(s_io_dma, 16)
                sp.dma_start(by_block(h_dram)[:, g, :], stage_one).then_inc(s_io_dma, 16)
                sp.wait_ge(nodes["io"]["used"], BG * i + BG + 2)
                sp.sem_inc(s_pass, 1)
                sp.dma_start(by_block(feat_in_dram)[:, g, :], io_stage[:, :, 0:D]).then_inc(s_io_dma, 16)
                sp.dma_start(by_block(feat_out_dram)[:, g, :], io_stage[:, :, D:2 * D]).then_inc(s_io_dma, 16)
                sp.wait_ge(s_io_dma, 64 * i + 64)
                sp.sem_inc(s_pass, 1)
                sp.sem_inc(s_stored, 1)

            for s in s_scat["src"]:
                sp.wait_ge(s, 16 * U * (T0 // UT))
            sp.wait_ge(s_srt_used, 1)
            srt_s = srt[:, :, :].rearrange("p t f -> p (t f)")[:, 0:T * FS]
            sp.dma_start(srt_s, rec_src_dram.rearrange("(p t) f -> p (t f)", p=P)
                         ).then_inc(loops["out"]["srt"], 16)

            sp.wait_ge(loops["out"]["sums"], R + T // U)
            out_full = out[0:(NB - 1) * P, :].rearrange("(b p) f -> p b f", p=P)

            def fetch(i):
                g = bass.ds(BG * i, BG)
                sp.dma_start(xin, by_block(x1_dram)[:, g, :]).then_inc(s_fin_in, 16)
                sp.dma_start(hin, by_block(h_dram)[:, g, :]).then_inc(s_fin_in, 16)
            with sp.Fori(0, NG - 1) as i:
                fetch(i)
                sp.wait_ge(s_out, i + 1)
                sp.sem_inc(s_pass, 1)
                sp.dma_start(out_full[:, bass.ds(BG * i, BG), :], xin).then_inc(s_out_dma, 16)
                sp.wait_ge(s_out_dma, 16 * i + 16)
                sp.sem_inc(s_pass, 1)
            fetch(NG - 1)
            sp.wait_ge(s_out, NG)
            sp.dma_start(out_full[:, BG * (NG - 1):NB - 1, :], xin[:, 0:BG - 1, :]).then_inc(s_out_dma, 16)
            rest = N - (NB - 1) * P
            sp.dma_start(out[(NB - 1) * P:N, :], xin[0:rest, BG - 1, :]).then_inc(s_out_dma, 16)
            sp.wait_ge(s_out_dma, 16 * (NG + 1))

        @block.gpsimd
        def _(pool):
            own = Chain(pool, s_pool)
            nc.gpsimd.memset(zeros, 0.0).then_inc(s_zero, 1)
            own.ordered(nc.gpsimd.memset(ones[:], 1.0))
            own.ordered(nc.gpsimd.memset(tri[:], 1.0))
            own.ordered(nc.gpsimd.memset(ident[:], 0.0))
            nc.gpsimd.memset(eps[:], EPS)
            own.ordered(nc.gpsimd.affine_select(out=tri[:], in_=tri[:], compare_op=ALU.is_gt, fill=0.0,
                                                base=0, pattern=[[1, P]], channel_multiplier=-1))
            own.ordered(nc.gpsimd.affine_select(out=ident[:], in_=ident[:], compare_op=ALU.not_equal,
                                                fill=1.0, base=0, pattern=[[1, P]], channel_multiplier=-1))
            nc.gpsimd.iota(iota_row[:], pattern=[[1, P]], base=0, channel_multiplier=0,
                           allow_small_or_imprecise_dtypes=True)
            own.ordered(nc.gpsimd.iota(iota_pair, pattern=[[1, PAIRS]], base=0, channel_multiplier=0,
                                       allow_small_or_imprecise_dtypes=True))
            pool.sem_inc(s_const, 1)

            def wait_here(s, v):
                pool.wait_ge(s, v)
                pool.sem_inc(s_pass, 1)

            pool.wait_ge(s_zeroed, 6 * 16)
            for n, (key, dram, f) in enumerate((("dst", rec_dst_dram, FD), ("src", rec_src_dram, FS))):
                with pool.Fori(0, T0 // UT) as i:
                    for r in range(R):
                        wait_here(s_rec, (n * (T0 // U) + R * i) + r + 1)
                        for u in range(U):
                            pool.indirect_dma_start(
                                out=dram, out_offset=bass.IndirectOffsetOnAxis(
                                    ap=idx_stage[:, r, u:u + 1], axis=0),
                                in_=stage_scatter[:, r, u, 0:f], in_offset=None,
                            ).then_inc(s_scat[key][r], 16)

            def gathers(k, table, free):
                with pool.Fori(0, T // UT) as i:
                    for r in range(R):
                        wait_here(k["idx"], R * i + r + 1)
                        for s in free:
                            wait_here(s, R * i + r + 1)
                        for u in range(U):
                            pool.indirect_dma_start(
                                out=rows_buf[:, U * r + u, :], out_offset=None, in_=table,
                                in_offset=bass.IndirectOffsetOnAxis(ap=idx_stage[:, r, u:u + 1], axis=0),
                            ).then_inc(k["got"][r], 16)

            gathers(loops["l0"], x, (loops["l0"]["sums"],))
            for name, table in (("in", feat_in_dram), ("out", feat_out_dram)):
                k = loops[name]
                pool.wait_ge(s_stored, NG + 1)
                gathers(k, table, (k["sums"],))

        @block.scalar
        def _(act):
            act.wait_ge(s_const, 1)
            rad_v = rad.rearrange("p (s t) -> p s t", s=2)
            with act.Fori(0, NSUB // 2) as i:
                for h in range(2):
                    act.wait_ge(s_hid_ps, 2 * i + h + 1)
                    for q in range(2):
                        ins = nc.scalar.activation(hidden[:, q, :], ps[q][:, :], ACT.Silu,
                                                   scale=1.0 / 10.0 ** 0.5)
                    ins.then_inc(s_hid, 1)
                    act.wait_ge(s_rad_ps, 2 * i + h + 1)
                    nc.scalar.copy(rad_v[:, :, bass.ds((2 * i + h) * (ESUB // P), ESUB // P)],
                                   ps[2][:, 0:2 * ESUB // P].rearrange("p (t s) -> p s t", s=2)
                                   ).then_inc(s_rad, 1)
            k = loops["l0"]
            act.wait_ge(k["srt"], 16)
            with act.Fori(0, T // UT) as i:
                for r in range(R):
                    act.wait_ge(k["got"][r], 16 * U * (i + 1))
                    act.wait_ge(k["sums"], R * i + r + R - 1)
                    for u in range(U - 1):
                        for m in range(3):
                            cm = srt[:, bass.ds(UT * i + U * r + u, 1), SW + 1 + m]
                            nc.scalar.activation(msg[:, 0, r % 2, u, MUL * m:MUL * m + MUL],
                                                 rows_buf[:, U * r + u, 0:MUL], ACT.Copy, scale=cm)
                    act.wait_ge(s_flags, R * i + r + 1)
                    for u in range(U):
                        c0 = srt[:, bass.ds(UT * i + U * r + u, 1), SW]
                        ins = nc.scalar.activation(onehot_c0[:, r % 2, u, :], onehot[:, r % 2, u, :],
                                                   ACT.Copy, scale=c0)
                    ins.then_inc(k["scaled"], 1)

            def copy_turned(st, i, j, width):
                act.wait_ge(st["turns"], BG * i + j + 1)
                act.wait_ge(st["sums"], BG * i + j + before(j))
                to = turned[j % 2]
                if width > 512:
                    nc.scalar.copy(to[:, 512:width], ps[2 + j % 2][:, 0:width - 512])
                nc.scalar.copy(to[:, 0:min(512, width)], ps[j % 2][:, 0:min(512, width)]
                               ).then_inc(st["copied"], 1)

            def deviations(st, i):
                act.wait_ge(st["var"], i + 1)
                nc.scalar.activation(rstd[:, :], mv[:, :, 1:2].rearrange("p b o -> p (b o)"), ACT.Sqrt,
                                     bias=eps[:, 0:1]).then_inc(st["sd"], 1)

            with act.Fori(0, NG) as i:
                for j in range(BG):
                    copy_turned(nodes["l0"], i, j, 512)
                deviations(nodes["l0"], i)
            act.wait_ge(s_bnv, 1)
            nc.scalar.activation(bn_sd, bn_var, ACT.Sqrt, bias=eps[:, 0:1]).then_inc(s_bnsd, 1)
            with act.Fori(0, NG) as i:
                for j in range(BG):
                    copy_turned(nodes["io"], i, j, 256)
            st = nodes["fin"]
            with act.Fori(0, NG) as i:
                for j in range(BG + 1):
                    if j < BG:
                        copy_turned(st, i, j, 768)
                    if j >= 1:
                        n = j - 1
                        act.wait_ge(s_pre, BG * i + n + 1)
                        act.wait_ge(s_mixed, BG * i + n + before(n))
                        nc.scalar.activation(gates[:, n % 2, 0:D], ps[4 + n % 2][:, 0:D], ACT.Sigmoid)
                        nc.scalar.activation(gates[:, n % 2, D:2 * D], ps[4 + n % 2][:, D:2 * D],
                                             ACT.Tanh).then_inc(st["used"], 1)
                deviations(st, i)

        @block.tensor
        def _(pe):
            pe.wait_ge(s_in["weights"], 8 * 16)
            pe.sem_inc(s_emb_free, 2)
            pe.sem_inc(s_rad, 1)
            with pe.Fori(0, NSUB // 2) as i:
                for h in range(2):
                    pe.wait_ge(s_emb[h], 16 * (i + 1))
                    pe.wait_ge(s_rad, 2 * i + h + 1)
                    for q in range(2):
                        ins = pe.matmul(ps[q][:, :], fc1_bd[:, :], emb_sb[:, h, 512 * q:512 * q + 512],
                                        start=True, stop=True)
                    ins.then_inc(s_hid_ps, 1)
                    pe.wait_ge(s_hid, 2 * i + h + 1)
                    for q in range(2):
                        for t in range(4):
                            c = 2 * (4 * q + t)
                            ins = pe.matmul(ps[2][:, c:c + 2], hidden[:, q, P * t:P * t + P], fc2_bd[:, :],
                                            start=True, stop=True)
                    ins.then_inc(s_rad_ps, 1)
                    pe.sem_inc(s_emb_free, 1)
            pe.wait_ge(s_const, 1)
            for n in range(2):
                pe.wait_ge(s_cnt, n + 1)
                pe.matmul(ps[3][:, 0:NB], tri[:, :], small[:, 0, 0:NB], start=True, stop=True)
                pe.matmul(ps[4][:, 0:NB], ones[:, :], small[:, 0, 0:NB], start=True, stop=True
                          ).then_inc(s_cnt_ps, 1)
                pe.wait_ge(s_tend, n + 1)
                pe.matmul(ps[3][0:NB, 0:1], small[0:1, 2, 0:NB], ones[0:1, 0:1], start=True, stop=True
                          ).then_inc(s_tend_ps, 1)
                pe.wait_ge(s_past, n + 1)
                pe.matmul(ps[3][:, 0:PAIRS], ones[0:NB, :], past[0:NB, :], start=True, stop=True
                          ).then_inc(s_past_ps, 1)

            def edge_sums(k, ready, products):
                with pe.Fori(0, T // UT) as i:
                    for r in range(R):
                        for s, v in ready(i, r):
                            pe.wait_ge(s, v)
                        pe.wait_ge(k["added"], 2 * (R * i + r) + 2)
                        for u in range(U):
                            parts = products(r, u)
                            for c, (hot, rows, at, width) in enumerate(parts):
                                ins = pe.matmul(ps[2 * r + u // 2][:, at:at + width], hot, rows,
                                                start=u % 2 == 0 and c == 0,
                                                stop=u % 2 == 1 and c == len(parts) - 1,
                                                skip_group_check=True)
                        ins.then_inc(k["sums"], 1)

            k0 = loops["l0"]
            edge_sums(k0, lambda i, r: ((k0["hot"], R * i + r + 2), (k0["scaled"], R * i + r + 1)),
                      lambda r, u: ((onehot_c0[:, r % 2, u, :], rows_buf[:, U * r + u, :], 0, D),
                                    (onehot[:, r % 2, u, :], msg[:, 0, r % 2, u, :], D, D)))

            def products(st, turn, product, ready):
                with pe.Fori(0, NG) as i:
                    for s, per in ready:
                        pe.wait_ge(s, per * (i + 1))
                    for j in range(BG + 1):
                        if j < BG:
                            pe.wait_ge(st["copied"], BG * i + j + before(j))
                            turn(j).then_inc(st["turns"], 1)
                        if j >= 1:
                            n = j - 1
                            pe.wait_ge(st["copied"], BG * i + n + 1 + 2)
                            pe.wait_ge(st["used"], BG * i + n + before(n))
                            product(n).then_inc(st["sums"], 1)

            def turn(parts, first_bank):
                for c, of in enumerate(parts):
                    ins = pe.transpose(ps[first_bank][:, P * c:P * c + P], of, ident[:, :])
                return ins

            def halves(v):
                return [v[:, 0:P], v[:, P:D]]

            def weights0(j):
                for c in range(4):
                    ins = pe.matmul(ps[4 + j % 2][:, MUL * c:MUL * c + MUL], turned[j % 2][:, P * c:P * c + P],
                                    (w_odd if c else w_even)[:, :], start=True, stop=True)
                return ins

            def weights(parts):
                def product(j):
                    for c, w in enumerate(parts):
                        ins = pe.matmul(ps[4 + j % 2][:, :], turned[j % 2][:, P * c:P * c + P], w,
                                        start=c == 0, stop=c == len(parts) - 1)
                    return ins
                return product

            pe.wait_ge(s_wconst, 1)
            products(nodes["l0"], lambda j: turn([stage[:, j, P * c:P * c + P] for c in range(4)], j % 2),
                     weights0, ((nodes["l0"]["staged"], 1),))

            acc_v = acc[:, :].rearrange("p (b f) -> p b f", b=NB)
            pe.wait_ge(s_x1, NG + 1)
            pe.matmul(ps[6][:, 0:D], ones[:, :], acc_v[:, 0, 0:D], start=True, stop=False)
            with pe.Fori(1, NB - 1) as b:
                pe.matmul(ps[6][:, 0:D], ones[:, :], acc_v[:, bass.ds(b, 1), 0:D].rearrange("p a f -> p (a f)"),
                          start=False, stop=False)
            pe.matmul(ps[6][:, 0:D], ones[:, :], acc_v[:, NB - 1, 0:D], start=False, stop=True
                      ).then_inc(s_sum_ps, 1)

            def squares(first, last):
                for j in range(BG):
                    ins = pe.matmul(ps[7][:, 0:D], ones[:, :], stage_one[:, j, :],
                                    start=first and j == 0, stop=last and j == BG - 1)
                ins.then_inc(s_sq_ps, 1)
            pe.wait_ge(s_sq, 1)
            squares(True, False)
            with pe.Fori(1, NG - 1) as i:
                pe.wait_ge(s_sq, i + 1)
                squares(False, False)
            pe.wait_ge(s_sq, NG)
            squares(False, True)

            products(nodes["io"], lambda j: turn(halves(stage_one[:, j, :]), j % 2),
                     weights([wio[:, 0, :], wio[:, 1, :]]), ((nodes["io"]["staged"], 1),))

            for name in ("in", "out"):
                k1 = loops[name]
                edge_sums(k1, lambda i, r: ((k1["hot"], R * i + r + 1), (k1["got"][r], 16 * U * (i + 1))),
                          lambda r, u: ((onehot[:, r % 2, u, :], rows_buf[:, U * r + u, :], 0, D),))

            def turn_fin(j):
                turn(halves(hin[:, j, :]), 2 + j % 2)
                return turn(halves(stage_one[:, j, :]) + halves(stage_two[:, j, :]), j % 2)
            products(nodes["fin"], turn_fin, weights([wx[:, c, :] for c in range(6)]),
                     ((nodes["fin"]["staged"], 1), (s_fin_in, 32)))

        @block.vector
        def _(dve):
            own = Chain(dve, s_dve)
            V = nc.vector
            for k in loops.values():
                dve.sem_inc(k["added"], LAG)
                dve.sem_inc(k["sums"], R)
            for st in nodes.values():
                for name in ("copied", "sums", "used"):
                    dve.sem_inc(st[name], 2)
            dve.sem_inc(s_mixed, 2)
            dve.sem_inc(loops["l0"]["hot"], 1)
            own.step(V.memset(block_dst[:, :], 0))
            own.step(V.memset(block_src[:, :], 0))
            own.step(V.memset(srt[:, T:T + UT, :], 0.0))
            own.step(V.memset(stage_scatter[:, :, :, :], 0.0))
            own.step(V.memset(rec_dst[:, :, FD - 1:FD], 0.0))
            own.ordered(V.memset(rec_src[:, :, FS - 1:FS], 0.0))
            dve.wait_ge(s_const, 1)

            cnt, tend, tiles, tstart, base = (small[:, q, 0:NB] for q in (0, 2, 1, 3, 4))
            int_a, int_b = (small[:, q, 0:NB].bitcast(I32) for q in (5, 6))

            def positions(n, key, landed, rec, addr, table):
                dve.wait_ge(landed, 16)
                own.ordered(V.tensor_scalar(tmp_i, key, 7, None, ALU.arith_shift_right))
                own.ordered(V.tensor_copy(blk_f, tmp_i))
                own.ordered(V.tensor_scalar(tmp_i, key, 127, None, ALU.bitwise_and))
                own.step(V.tensor_copy(rec[:, :, SLOC], tmp_i))
                own.ordered(V.memset(rank, 0.0))
                with dve.Fori(0, NB) as b:
                    own.loop(b, 5)
                    own.ordered(V.tensor_scalar(hot, blk_f, iota_row[:, bass.ds(b, 1)], None, ALU.is_equal))
                    own.ordered(V.tensor_tensor_scan(scan, hot, hot, 0.0, ALU.add, ALU.max))
                    own.step(V.tensor_copy(small[:, 0, bass.ds(b, 1)], scan[:, T0 - 1:T0]))
                    own.ordered(V.tensor_tensor(tmp_f, hot, scan, ALU.mult))
                    own.ordered(V.tensor_tensor(rank, rank, tmp_f, ALU.add))
                    own.end(NB)
                dve.sem_inc(s_cnt, 1)
                dve.wait_ge(s_cnt_ps, n + 1)
                own.ordered(V.tensor_scalar(int_a, ps[4][:, 0:NB], float(2 * P - 1), None, ALU.add))
                own.ordered(V.tensor_scalar(int_b, int_a, PAIR_BITS, None, ALU.arith_shift_right))
                own.ordered(V.tensor_copy(tiles, int_b))
                own.ordered(V.tensor_tensor_scan(tend, tiles, tiles, 0.0, ALU.add, ALU.max))
                own.ordered(V.tensor_tensor(tstart, tend, tiles, ALU.subtract))
                own.ordered(V.scalar_tensor_tensor(out=base, in0=tstart, scalar=2.0 * P, in1=ps[3][:, 0:NB],
                                                   op0=ALU.mult, op1=ALU.add))
                own.ordered(V.tensor_scalar(base, base, -1.0, None, ALU.add))
                dve.sem_inc(s_tend, 1)
                dve.wait_ge(s_tend_ps, n + 1)
                own.ordered(V.tensor_copy(small[0:NB, 7, 0:1], ps[3][0:NB, 0:1]))
                own.ordered(V.tensor_scalar(past[0:NB, :], iota_pair[0:NB, :], small[0:NB, 7, 0:1], None, ALU.is_ge))
                dve.sem_inc(s_past, 1)
                dve.wait_ge(s_past_ps, n + 1)
                own.ordered(V.tensor_scalar(table[0:1, LAG:LAG + PAIRS], ps[3][0:1, 0:PAIRS],
                                            float(NB - 1), None, ALU.min))
                with dve.Fori(0, NB) as b:
                    own.loop(b, 2)
                    own.ordered(V.tensor_scalar(tmp_f, blk_f, iota_row[:, bass.ds(b, 1)],
                                                small[:, 4, bass.ds(b, 1)], ALU.is_equal, ALU.mult))
                    own.ordered(V.tensor_tensor(rank, rank, tmp_f, ALU.add))
                    own.end(NB)
                own.ordered(V.tensor_copy(tmp_i, rank))
                own.ordered(V.tensor_scalar(addr, tmp_i, 7, None, ALU.arith_shift_right))
                own.ordered(V.tensor_copy(scan, addr))
                own.ordered(V.tensor_scalar(addr, tmp_i, 127, None, ALU.bitwise_and))
                own.ordered(V.tensor_copy(hot, addr))
                own.ordered(V.scalar_tensor_tensor(out=addr, in0=hot, scalar=float(T), in1=scan,
                                                   op0=ALU.mult, op1=ALU.add))

            positions(0, key_dst, s_in["dst"], rec_dst, addr_dst, block_dst)
            dve.wait_ge(s_in["src"], 16)
            dve.wait_ge(s_in["attr"], 48)
            dve.wait_ge(s_rad, 1 + NSUB)
            own.step(V.tensor_copy(rec_dst[:, :, DIN].bitcast(I32), key_src))
            own.step(V.tensor_copy(rec_src[:, :, DIN].bitcast(I32), key_dst))
            for c in range(4):
                own.step(V.scalar_tensor_tensor(out=rec_dst[:, :, SW + c], in0=attr[:, :, c],
                                                scalar=SILU_NORM / 8.0, in1=rad, op0=ALU.mult, op1=ALU.mult))
            own.step(V.tensor_copy(rec_dst[:, :, WIN], iw_sb))
            own.ordered(V.tensor_copy(rec_src[:, :, SW], ow_sb))

            def scatter_stage(key, rec, addr, f):
                def unit(i, r):
                    t = bass.ds(UT * i + U * r, U) if not isinstance(i, int) else slice(UT * i + U * r, UT * i + U * r + U)
                    V.tensor_copy(idx_stage[:, r, :], addr[:, t])
                    V.tensor_copy(stage_scatter[:, r, :, 0:f], rec[:, t, :]).then_inc(s_rec, 1)
                for r in range(R):
                    unit(0, r)
                with dve.Fori(1, T0 // UT) as i:
                    for r in range(R):
                        dve.wait_ge(s_scat[key][r], 16 * U * i)
                        unit(i, r)
            scatter_stage("dst", rec_dst, addr_dst, FD)
            positions(1, key_src, s_in["src"], rec_src, addr_src, block_src)
            for r in range(R):
                dve.wait_ge(s_scat["dst"][r], 16 * U * (T0 // UT))
            scatter_stage("src", rec_src, addr_src, FS)
            for r in range(R):
                dve.wait_ge(s_scat["src"][r], 16 * U * (T0 // UT))

            dve.wait_ge(s_in["rows"], 16 * 19)
            alpha = (2.0 * MUL) ** -0.5 / 4.0
            own.step(V.tensor_scalar(w_odd[:, :], w_odd[:, :], alpha, None, ALU.mult))
            own.step(V.tensor_scalar(w_even[0:64, :], w_even[0:64, :], alpha, None, ALU.mult))
            own.ordered(V.tensor_scalar(w_even[64:128, :], w_even[64:128, :], alpha * 3.0 ** -0.5, None, ALU.mult))
            dve.sem_inc(s_wconst, 1)

            def edge_loop(k, rec, table, width, offset, first, second, per):
                if k is not loops["in"]:
                    dve.wait_ge(k["srt"], 16)
                index = rec[:, :, DIN].bitcast(I32)
                for r in range(R):
                    V.tensor_copy(idx_stage[:, r, :], index[:, U * r:U * r + U]).then_inc(k["idx"], 1)

                def load_blocks(place, n):
                    regs = block_regs[:n]
                    dve.load(regs, table[0:1, bass.ds(place, n)])
                    return [dve.snap(r, min_val=0, max_val=NB - 1) for r in regs]

                def add(blk, bank, count):
                    to = acc[:, bass.ds(blk * width + offset, width)]
                    dve.wait_ge(k["added"], count)
                    V.tensor_tensor(to, to, ps[bank][:, 0:width], ALU.add).then_inc(k["added"], 1)

                for q in range(LAG):
                    V.memset(ps[8 - LAG + q][:, 0:width], 0.0)
                own.ordered(V.memset(acc[:, offset:offset + NB * width], 0.0))
                with dve.Fori(0, T // UT) as i:
                    own.loop(i, R * per)
                    blocks = load_blocks(2 * R * i, 2 * R)
                    for r in range(R):
                        dve.wait_ge(k["sums"], R * i + r + R - 1)
                        first(i, r)
                        dve.wait_ge(k["got"][r], 16 * U * (i + 1))
                        V.tensor_copy(idx_stage[:, r, :], index[:, bass.ds(UT * i + UT + U * r, U)]
                                      ).then_inc(k["idx"], 1)
                        second[0](i, r)
                        bank, count = 2 * ((r + 2) % R), LAG + 2 * (R * i + r)
                        add(blocks[2 * r], bank, count)
                        second[1](i, r)
                        add(blocks[2 * r + 1], bank + 1, count + 1)
                    own.end(T // UT)
                dve.wait_ge(k["sums"], R + T // U)
                last = load_blocks(PAIRS, LAG)
                for q in range(LAG):
                    add(last[q], 8 - LAG + q, LAG + PAIRS + q)
                dve.wait_ge(k["added"], 2 * LAG + PAIRS)

            block_regs = [dve.alloc_register(f"block{q}") for q in range(2 * R)]

            def unit_of(i, r):
                return rows_buf[:, U * r:U * r + U, :], bass.ds(UT * i + U * r, U)

            def flags0(i, r):
                g, t = unit_of(i, r)
                V.tensor_tensor(onehot[:, r % 2, :, :], srt[:, t, SLOC:SLOC + 1].to_broadcast([P, U, P]),
                                iota_row[:, :].unsqueeze(1).to_broadcast([P, U, P]), ALU.is_equal
                                ).then_inc(s_flags, 1)

            def products0(i, r):
                g, t = unit_of(i, r)
                s1 = g[:, :, MUL:D].rearrange("p u (i m) -> p u i m", m=3)
                dve.wait_ge(loops["l0"]["hot"], R * i + r + 1)
                own.step(V.tensor_tensor(prod[:, :, :, :], s1,
                                         srt[:, t, SW + 1:SW + 4].unsqueeze(2).to_broadcast([P, U, MUL, 3]),
                                         ALU.mult))

            def messages0(i, r):
                own.settle()
                last = srt[:, bass.ds(UT * i + U * r + U - 1, 1), SW + 1:SW + 4].rearrange("p a m -> p (a m)")
                V.tensor_tensor(msg[:, 0, r % 2, U - 1, 0:3 * MUL].rearrange("p (m i) -> p m i", m=3),
                                rows_buf[:, U * r + U - 1, 0:MUL].unsqueeze(1).to_broadcast([P, 3, MUL]),
                                last.unsqueeze(2).to_broadcast([P, 3, MUL]), ALU.mult)
                V.tensor_reduce(msg[:, 0, r % 2, :, 3 * MUL:D], prod[:, :, :, :], mybir.AxisListType.X, ALU.add
                                ).then_inc(loops["l0"]["hot"], 1)

            edge_loop(loops["l0"], srt, block_dst, 2 * D, 0, flags0, (products0, messages0), 1)

            acc_v = acc[:, :].rearrange("p (b f) -> p b f", b=NB)
            dve.sem_inc(s_x1, 1)

            def normalise(st, i, to):
                for j in range(BG):
                    own.step(V.bn_stats(stats[:, j, :], to[:, j, :]))
                own.settle()
                dve.sem_inc(s_pass, 1)
                for j in range(BG):
                    own.step(V.bn_aggr(mv[:, j, :], stats[:, j, :]))
                own.settle()
                dve.sem_inc(st["var"], 1)
                dve.wait_ge(st["sd"], i + 1)
                own.ordered(V.reciprocal(rstd[:, :], rstd[:, :]))

            st = nodes["l0"]
            with dve.Fori(0, NG) as i:
                own.loop(i, 8 + 2 * BG + 2 * BG + 1 + BG)
                group = bass.ds(BG * i, BG)
                own.step(V.tensor_copy(stage[:, :, 0:MUL], acc_v[:, group, 0:MUL]))
                own.step(V.tensor_copy(stage[:, :, MUL:P], acc_v[:, group, 7 * MUL:8 * MUL]))
                for m in range(3):
                    to = stage[:, :, P * (m + 1):P * (m + 2)]
                    own.step(V.tensor_copy(to[:, :, 0:MUL], acc_v[:, group, D + MUL * m:D + MUL * (m + 1)]))
                    own.step(V.tensor_copy(to[:, :, MUL:P], acc_v[:, group, MUL:D].rearrange(
                        "p b (i m) -> p b i m", m=3)[:, :, :, m]))
                own.settle()
                dve.sem_inc(st["staged"], 1)
                dve.wait_ge(s_xin, 16 * (i + 1))
                for j in range(BG):
                    dve.wait_ge(st["sums"], BG * i + j + 1 + 2)
                    y = ps[4 + j % 2]
                    own.step(V.tensor_tensor(xin[:, j, 0:MUL], xin[:, j, 0:MUL], y[:, 0:MUL], ALU.add))
                    v = xin[:, j, MUL:D].rearrange("p (o m) -> p m o", m=3)
                    own.ordered(V.tensor_tensor(v, v, y[:, MUL:D].rearrange("p (m o) -> p m o", m=3), ALU.add))
                    dve.sem_inc(st["used"], 1)
                normalise(st, i, xin)
                for j in range(BG):
                    own.step(V.tensor_scalar(acc_v[:, bass.ds(BG * i + j, 1), 0:D].rearrange("p a f -> p (a f)"),
                                             xin[:, j, :], mv[:, j, 0:1], rstd[:, j:j + 1], ALU.subtract, ALU.mult))
                own.settle()
                dve.sem_inc(s_x1, 1)
                own.end(NG)

            dve.wait_ge(s_sum_ps, 1)
            own.ordered(V.tensor_scalar(mean_row[:, :], ps[6][:, 0:D], 1.0 / N, None, ALU.mult))

            def squares(i):
                x1 = acc_v[:, bass.ds(BG * i, BG), 0:D] if not isinstance(i, int) else acc_v[:, 0:BG, 0:D]
                own.ordered(V.tensor_tensor(stage_one, x1, mean_row[:, :].unsqueeze(1).to_broadcast([P, BG, D]),
                                            ALU.subtract))
                own.ordered(V.tensor_tensor(stage_one, stage_one, stage_one, ALU.mult))
                dve.sem_inc(s_sq, 1)
            squares(0)
            with dve.Fori(1, NG) as i:
                dve.wait_ge(s_sq_ps, i)
                own.loop(i - 1, 2)
                squares(i)
                own.end(NG - 1)
            dve.wait_ge(s_sq_ps, NG)
            own.ordered(V.tensor_tensor(bn_sd, mean_row[:, :], mean_row[:, :], ALU.mult))
            own.ordered(V.scalar_tensor_tensor(out=bn_var, in0=bn_sd, scalar=-float(NP - N), in1=ps[7][:, 0:D],
                                               op0=ALU.mult, op1=ALU.add))
            own.ordered(V.tensor_scalar(bn_var, bn_var, 1.0 / N, None, ALU.mult))
            dve.sem_inc(s_bnv, 1)
            dve.wait_ge(s_bnsd, 1)
            own.ordered(V.reciprocal(bn_sd, bn_sd))
            own.ordered(V.tensor_tensor(bn_a[:, :], bn_a[:, :], bn_sd, ALU.mult))
            own.ordered(V.tensor_tensor(bn_sd, mean_row[:, :], bn_a[:, :], ALU.mult))
            own.ordered(V.tensor_tensor(bn_b[:, :], bn_b[:, :], bn_sd, ALU.subtract))

            st = nodes["io"]
            dve.sem_inc(s_stored, 1)
            with dve.Fori(0, NG) as i:
                own.loop(i, 2 + BG)
                x1 = acc_v[:, bass.ds(BG * i, BG), 0:D]
                dve.wait_ge(s_stored, i + 1)
                own.ordered(V.tensor_tensor(stage_one, x1, bn_a[:, :].unsqueeze(1).to_broadcast([P, BG, D]), ALU.mult))
                own.ordered(V.tensor_tensor(stage_one, stage_one, bn_b[:, :].unsqueeze(1).to_broadcast([P, BG, D]),
                                            ALU.add))
                dve.sem_inc(st["staged"], 1)
                for j in range(BG):
                    dve.wait_ge(st["sums"], BG * i + j + 1 + 2)
                    own.ordered(V.tensor_tensor(io_stage[:, j, :], ps[4 + j % 2][:, :], bias_io[:, :], ALU.add))
                    dve.sem_inc(st["used"], 1)
                own.end(NG)
            dve.wait_ge(s_stored, NG + 1)

            def layer1(name, rec, table, offset, w):
                def weighted(i, r):
                    for u in range(U):
                        t = bass.ds(UT * i + U * r + u, 1)
                        ins = V.tensor_scalar(onehot[:, r % 2, u, :], iota_row[:, :], rec[:, t, SLOC],
                                              rec[:, t, w], ALU.is_equal, ALU.mult)
                    ins.then_inc(loops[name]["hot"], 1)

                def nothing(i, r):
                    pass
                edge_loop(loops[name], rec, table, D, offset, weighted, (nothing, nothing), 0)
            layer1("in", srt, block_dst, 0, WIN)
            dve.sem_inc(s_srt_used, 1)
            srt_s = srt[:, :, :].rearrange("p t f -> p (t f)")[:, 0:(T + UT) * FS].rearrange("p (t f) -> p t f", f=FS)
            own.ordered(V.memset(srt_s[:, T:T + UT, :], 0.0))
            layer1("out", srt_s, block_src, NB * D, SW)

            st = nodes["fin"]
            a_in = acc[:, 0:NB * D].rearrange("p (b f) -> p b f", b=NB)
            a_out = acc[:, NB * D:2 * NB * D].rearrange("p (b f) -> p b f", b=NB)
            with dve.Fori(0, NG) as i:
                own.loop(i, 2 + 5 * BG + 2 * BG + 1 + BG)
                group = bass.ds(BG * i, BG)
                own.step(V.tensor_copy(stage_one, a_in[:, group, :]))
                own.ordered(V.tensor_copy(stage_two, a_out[:, group, :]))
                dve.sem_inc(st["staged"], 1)
                dve.wait_ge(s_fin_in, 32 * (i + 1))
                for j in range(BG + 1):
                    if j < BG:
                        y = ps[4 + j % 2]
                        dve.wait_ge(st["sums"], BG * i + j + 1 + 2)
                        own.ordered(V.tensor_tensor(y[:, :], y[:, :], bias_x[:, :], ALU.add))
                        dve.sem_inc(s_pre, 1)
                    if j >= 1:
                        n = j - 1
                        gate, new = gates[:, n % 2, 0:D], gates[:, n % 2, D:2 * D]
                        dve.wait_ge(st["used"], BG * i + n + 1 + 2)
                        own.ordered(V.tensor_tensor(hin[:, n, :], hin[:, n, :], new, ALU.subtract))
                        own.step(V.tensor_tensor(xin[:, n, :], xin[:, n, :], new, ALU.add))
                        own.ordered(V.tensor_tensor(hin[:, n, :], hin[:, n, :], gate, ALU.mult))
                        own.ordered(V.tensor_tensor(xin[:, n, :], xin[:, n, :], hin[:, n, :], ALU.add))
                        dve.sem_inc(s_mixed, 1)
                normalise(st, i, xin)
                for j in range(BG):
                    own.step(V.tensor_scalar(xin[:, j, :], xin[:, j, :], mv[:, j, 0:1], rstd[:, j:j + 1],
                                             ALU.subtract, ALU.mult))
                own.settle()
                dve.sem_inc(s_out, 1)
                own.end(NG)


def kernel(x, src, dst, edge_attr_10, edge_attr_4, edge_weight, edge_weight_n2,
           L0_gnn_w_00_0, L0_gnn_w_11_0, L0_gnn_w_01_1, L0_gnn_w_10_1, L0_gnn_fc_w1, L0_gnn_fc_w2,
           L1_gnn_gamma, L1_gnn_beta, L1_gnn_W_in, L1_gnn_b_in, L1_gnn_W_out, L1_gnn_b_out,
           L1_gnn_W_x2i, L1_gnn_b_x2i, L1_gnn_W_h2h):
    import numpy as np
    import concourse.bacc as bacc
    from concourse.bass_utils import run_bass_kernel_spmd

    EP = T0 * P

    def by_tile(a, fill=0):
        a = np.asarray(a)
        whole = np.full((EP,) + a.shape[1:], fill, a.dtype)
        whole[:E] = a
        whole = whole.reshape((T0, P) + a.shape[1:]).swapaxes(0, 1)
        return np.ascontiguousarray(whole.reshape(P, -1))

    emb = np.zeros((EP, 10), np.float32)
    emb[:E] = np.asarray(edge_attr_10)
    x_pad = np.zeros((NP, D), np.float32)
    x_pad[:N] = np.asarray(x)
    arrays = {
        "x": x_pad,
        "src_t": by_tile(src, N - 1), "dst_t": by_tile(dst, N - 1),
        "attr_t": by_tile(edge_attr_4), "iw_t": by_tile(edge_weight), "ow_t": by_tile(edge_weight_n2),
        "emb": np.ascontiguousarray(emb.reshape(2, EP // 2, 10).transpose(0, 2, 1).reshape(20, EP // 2)),
        "w00": L0_gnn_w_00_0, "w11": L0_gnn_w_11_0, "w01": L0_gnn_w_01_1, "w10": L0_gnn_w_10_1,
        "fc1": L0_gnn_fc_w1, "fc2": L0_gnn_fc_w2,
        "gamma": np.asarray(L1_gnn_gamma)[None], "beta": np.asarray(L1_gnn_beta)[None],
        "w_in": L1_gnn_W_in, "b_in": np.asarray(L1_gnn_b_in)[None],
        "w_out": L1_gnn_W_out, "b_out": np.asarray(L1_gnn_b_out)[None],
        "w_x2i": L1_gnn_W_x2i, "b_x2i": np.asarray(L1_gnn_b_x2i)[None], "w_h2h": L1_gnn_W_h2h,
    }
    nc = bacc.Bacc("TRN2", target_bir_lowering=False, num_devices=1)
    args, ins = [], {}
    for name, a in arrays.items():
        a = np.ascontiguousarray(np.asarray(a))
        ins["in_" + name] = a
        args.append(nc.dram_tensor("in_" + name, list(a.shape), mybir.dt.from_np(a.dtype),
                                   kind="ExternalInput").ap())
    result = nc.dram_tensor("out_0", [N, D], F32, kind="ExternalOutput").ap()
    build(nc, *args, result)
    r = run_bass_kernel_spmd(nc, [ins], core_ids=[0])
    return r.results[0]["out_0"]
```

```python
from contextlib import ExitStack

import concourse.bass as bass
from concourse import mybir

P = 128
N, E, D, MUL = 6250, 106250, 256, 64
NB = -(-N // P)
NP = NB * P
BG = 7
NG = NB // BG
T0 = 832
PAIRS = T0 // 2 + NB - 1
T = 2 * PAIRS
TS = T0 + NB - 1
HID = 64
PER = 8
STEPS = T0 // PER
COLS_IN = 4 * P
SRC_STEP = 6
SIGN_STEPS = 6
COUNTING = NB - 1
SORTING = 2
SORT_TURNS = 6
CNT, TEND, PADS, BASE, COLS, MISC, PAIRN, TSTART, INTS, SIGNS = 0, 2, 4, 5, 7, 8, 9, 11, 13, 16
U = 4
R = 4
UT = U * R
LAG = U
FD, FS = 8, 4
DIN, SLOC, SW = 0, 1, 2
WIN = 6
EPS = 1e-5
ACT_ZERO = 10240
SILU_NORM = 1.679177
assert NB == BG * NG and T % UT == 0 and TS % UT == 0 and T0 % UT == 0
assert STEPS % 8 == 0 and NB - 1 == 8 * SIGN_STEPS and NB == 8 * SORT_TURNS + 1

ALU = mybir.AluOpType
ACT = mybir.ActivationFunctionType
F32 = mybir.dt.float32
I32 = mybir.dt.int32


class Chain:

    def __init__(self, eng, sem):
        self.eng, self.sem, self.n, self.i, self.per = eng, sem, 0, None, 0

    def loop(self, i, per):
        self.i, self.per, self.base = i, per, self.n

    def end(self, trips):
        assert self.n - self.base == self.per, (self.n - self.base, self.per)
        self.n = self.base + trips * self.per
        self.i = None

    def step(self, ins):
        ins.then_inc(self.sem, 1)
        self.n += 1

    def settle(self):
        self.wait(0)

    def wait(self, later):
        n = self.n - later
        self.eng.wait_ge(self.sem, n if self.i is None else self.i * self.per + n)

    def ordered(self, ins):
        self.step(ins)
        self.settle()


def build(nc, x, src_t, dst_t, attr_t, iw_t, ow_t, emb, w00, w11, w01, w10, fc1, fc2,
          gamma, beta, w_in, b_in, w_out, b_out, w_x2i, b_x2i, w_h2h, out):
    with ExitStack() as ctx:
        def sb(name, shape, dt=F32):
            return ctx.enter_context(nc.sbuf_tensor(name, shape, dt))

        def sem(name):
            return ctx.enter_context(nc.semaphore(name))

        rec_dst_dram = nc.dram_tensor("rec_dst_list", [P * T, FD], F32, kind="Internal").ap()
        rec_src_dram = nc.dram_tensor("rec_src_list", [P * TS, FS], F32, kind="Internal").ap()
        feat_in_dram = nc.dram_tensor("feat_in", [NP, D], F32, kind="Internal").ap()
        feat_out_dram = nc.dram_tensor("feat_out", [NP, D], F32, kind="Internal").ap()
        gates_dram = nc.dram_tensor("gates_in", [NP, 2 * D], F32, kind="Internal").ap()
        x1_dram = nc.dram_tensor("x1", [NP, D], F32, kind="Internal").ap()
        h_dram = nc.dram_tensor("h", [NP, D], F32, kind="Internal").ap()

        acc = sb("acc", [P, NB * 2 * D])
        rows_buf = sb("rows_buf", [P, R * U, D])
        msg = sb("msg", [P, 2, 2, U, D])
        onehot = sb("onehot", [P, 2, U, P])
        onehot_c0 = sb("onehot_c0", [P, 2, U, P])
        prod = sb("prod", [P, U, MUL, 3])
        srt = sb("srt", [P, T + UT, FD])
        idx_stage = sb("idx_stage", [P, R, U], I32)
        stage_scatter = sb("stage_scatter", [P, R, U, FD])
        block_dst = sb("block_dst", [1, LAG + PAIRS + LAG], I32)
        block_src = sb("block_src", [1, LAG + TS + LAG], I32)
        start_dst = sb("start_dst", [1, PAIRS], I32)
        base_row = sb("base_row", [P, PAIRS + 2 * R])
        rec_src = sb("rec_src", [P, T0, FS])
        addr_src = sb("addr_src", [P, T0], I32)
        wio = sb("wio", [P, 2, 2 * D])
        w_even = sb("w_even", [P, MUL])
        w_odd = sb("w_odd", [P, MUL])
        ident = sb("ident", [P, P])
        ones = sb("ones", [P, P])
        tri = sb("tri", [P, P])
        iota_row = sb("iota_row", [P, P])
        bias_io = sb("bias_io", [P, 2 * D])
        bn_a = sb("bn_a", [P, D])
        bn_b = sb("bn_b", [P, D])
        stats = sb("stats", [P, BG, 6])
        mv = sb("mv", [P, BG, 2])
        rstd = sb("rstd", [P, BG])
        eps = sb("eps", [P, 1])
        zero = sb("zero", [P, 1])
        half_row = sb("half_row", [P, 64])
        fc2_row = sb("fc2_row", [P, HID])
        ps = [ctx.enter_context(nc.psum_tensor(f"ps{k}", [P, 512], F32)) for k in range(8)]

        at = [0]

        def part(words, dt=F32):
            v = acc[:, at[0]:at[0] + words]
            at[0] += words
            return v.bitcast(dt) if dt != F32 else v
        key_dst, key_src = part(T0 + 1, I32), part(T0, I32)
        attr = part(4 * T0).rearrange("p (t k) -> p t k", k=4)
        iw_sb, ow_sb = part(T0), part(T0)
        rec_dst = part(FD * T0).rearrange("p (t f) -> p t f", f=FD)
        rad = part(T0)
        blk_dst, blk_src = part(T0 + 1), part(T0)
        flags, places = ([part(T0) for _ in range(2)] for _ in range(2))
        counts = [part(T0), None]
        rank, tmp_f, tmp_g = part(T0), part(T0), flags[1]
        counts[1] = part(T0 + 1)
        counts[1], key_dst_blk = counts[1][:, 0:T0], counts[1].bitcast(I32)
        small = part(17 * 64).rearrange("p (q b) -> p q b", q=17)
        sign_out = [part(T0), tmp_f]
        tmp_i, addr_dst = sign_out[0].bitcast(I32), places[1].bitcast(I32)
        assert at[0] <= NB * 2 * D
        emb_sb = rows_buf[0:10 * PER, 0:4, :].rearrange("p a b -> p (a b)").rearrange(
            "p (h e) -> p h e", h=2)
        fc1_bd = prod[:, :, :, :].rearrange("p u i m -> p (u i m)")[0:10 * PER, 0:PER * HID]
        hidden = msg[:, 0].rearrange("p a u f -> p (a u f)").rearrange("p (q e) -> p q e", q=4)
        iota_pair = msg[:, 1].rearrange("p a u f -> p (a u f)")[:, 0:TS]
        past = [msg[:, 1].rearrange("p a u f -> p (a u f)")[:, TS:TS + PAIRS],
                onehot[:, :, :, :].rearrange("p a u f -> p (a u f)")[:, 0:TS]]
        zeros = rows_buf[:, 8:16, :].rearrange("p a b -> p (a b)")
        rows_flat = rows_buf[:, :, :].rearrange("p a b -> p (a b)")
        msg_flat = msg[:, :, :, :, :].rearrange("p a b u f -> p (a b u f)")
        stage = msg_flat[:, 0:BG * 2 * D].rearrange("p (b f) -> p b f", b=BG)
        stage_one = msg_flat[:, 0:BG * D].rearrange("p (b f) -> p b f", b=BG)
        io_stage = rows_flat[:, 0:BG * 2 * D].rearrange("p (b f) -> p b f", b=BG)
        xin = rows_flat[:, 0:BG * D].rearrange("p (b f) -> p b f", b=BG)
        gates = onehot_c0[:, :, :, :].rearrange("p a u f -> p a (u f)")
        srt_src = msg_flat[:, 0:(TS + UT) * FS].rearrange("p (t f) -> p t f", f=FS)
        srt_flat = srt[:, :, :].rearrange("p t f -> p (t f)")
        wx = srt_flat[:, 0:12 * D].rearrange("p (c f) -> p c f", c=6)
        bias_x = srt_flat[:, 12 * D:14 * D]
        h_blk, pre_blk = srt_flat[:, 14 * D:15 * D], srt_flat[:, 15 * D:17 * D]
        a_blk = srt_flat[:, (17 + BG) * D:(18 + BG) * D]
        h_ring = srt_flat[:, 17 * D:(17 + BG) * D].rearrange("p (b f) -> p b f", b=BG)
        rec_src_flat = rec_src[:, :, :].rearrange("p t f -> p (t f)")
        pre_ring = [rec_src_flat[:, 2 * D * j:2 * D * (j + 1)] for j in range(BG - 1)] + [
            srt_flat[:, (18 + BG) * D:(20 + BG) * D]]
        disorder = small[:, 15, 0:1].bitcast(I32)
        mean_row = gates[:, 1, 0:D]
        bn_sd, bn_var = gates[:, 0, 0:D], gates[:, 0, D:2 * D]
        turned = [onehot[:, :, :, :].rearrange("p a u f -> p (a u f)")[:, 0:3 * D],
                  prod[:, :, :, :].rearrange("p u i m -> p (u i m)")[:, 0:3 * D]]

        s_in = {k: sem(f"s_in_{k}") for k in ("dst", "src", "attr", "weights", "rows")}
        s_blk, s_signs = sem("s_blk"), sem("s_signs")
        s_emb = [sem(f"s_emb{h}") for h in range(2)]
        s_hid_ps = sem("s_hid_ps")
        s_hid = sem("s_hid")
        s_weighed = sem("s_weighed")
        s_rad = sem("s_rad")
        s_const = sem("s_const")
        s_wconst = sem("s_wconst")
        s_cnt, s_cnt_ps = ({k: sem(f"{n}_{k}") for k in ("dst", "src")}
                           for n in ("s_cnt", "s_cnt_ps"))
        s_tend, s_tend_ps = sem("s_tend"), sem("s_tend_ps")
        s_past, s_past_ps = sem("s_past"), sem("s_past_ps")
        s_tables = sem("s_tables")
        s_placed, s_ranked = sem("s_placed"), sem("s_ranked")
        s_dve_branch, s_pool_branch = sem("s_dve_branch"), sem("s_pool_branch")
        s_addr_dst, s_addr_src = sem("s_addr_dst"), sem("s_addr_src")
        s_recs_made = sem("s_recs_made")
        s_list = sem("s_list")
        s_pairs = sem("s_pairs")
        s_wx = sem("s_wx")
        s_read = sem("s_read")
        s_scattered = sem("s_scattered")
        s_acc_free = sem("s_acc_free")
        s_zero_acc = sem("s_zero_acc")
        s_zero = sem("s_zero")
        s_zeroed = sem("s_zeroed")
        s_scat = {k: [sem(f"s_scat_{k}{r}") for r in range(2)] for k in ("dst", "src")}
        s_dve, s_pool, s_act = sem("s_dve"), sem("s_pool"), sem("s_act")
        loops = {}
        for k in ("l0", "in", "out"):
            loops[k] = dict(
                idx=sem(f"s_idx_{k}"),
                got=[sem(f"s_got_{k}{r}") for r in range(R)],
                hot=sem(f"s_hot_{k}"),
                scaled=sem(f"s_scaled_{k}"),
                sums=sem(f"s_sums_{k}"),
                added=sem(f"s_added_{k}"),
            )
        s_flags = sem("s_flags")
        s_srt_used = sem("s_srt_used")
        s_srt_src = sem("s_srt_src")
        s_reads = sem("s_reads")
        nodes = {name: {q: sem(f"s_node_{q}_{name}") for q in
                        ("staged", "turns", "copied", "sums", "used", "var", "sd")}
                 for name in ("l0", "io", "fin")}
        s_xin, s_x1 = sem("s_xin"), sem("s_x1")
        s_sum_ps, s_sq, s_sq_ps = sem("s_sum_ps"), sem("s_sq"), sem("s_sq_ps")
        s_bnv, s_bnsd = sem("s_bnv"), sem("s_bnsd")
        s_stored, s_io_dma = sem("s_stored"), sem("s_io_dma")
        part_in = {q: sem(f"s_part_{q}") for q in ("h", "staged", "turns", "copied", "sums", "made", "out")}
        s_x1_in = sem("s_x1_in")
        s_ring = [sem(f"s_ring{j}") for j in range(BG)]
        s_stats = sem("s_stats")
        s_x1_new = sem("s_x1_new")
        s_pre, s_mixed = sem("s_pre"), sem("s_mixed")
        s_out, s_out_dma = sem("s_out"), sem("s_out_dma")

        def before(j):
            return 2 if j == 0 else 1

        s_pass = sem("s_pass")

        def place_of(n, kind):
            if kind == "l0":
                return n, 0
            return n // 2 % 4, D * (n % 2)

        block = ctx.enter_context(nc.Block())

        def by_block(dram):
            return dram.rearrange("(b p) f -> p b f", p=P)

        @block.sync
        def _(sp):
            sp.dma_start(key_dst, dst_t).then_inc(s_in["dst"], 16)
            sp.dma_start(key_src, src_t).then_inc(s_in["src"], 16)
            sp.dma_start(fc2_row[:, :], fc2.rearrange("i o -> o i").to_broadcast([P, HID])
                         ).then_inc(s_in["weights"], 16)
            sp.wait_ge(s_zero, 1)
            for j in range(PER):
                sp.dma_start(fc1_bd[10 * j:10 * j + 10, HID * j:HID * j + HID], fc1).then_inc(s_in["weights"], 16)
            def embeddings(i):
                for h in range(2):
                    sp.wait_ge(s_hid_ps, 8 * i + 4 * h + 4)
                    sp.sem_inc(s_pass, 1)
                    at = (2 * i + h) * COLS_IN
                    of = emb[:, at:at + COLS_IN] if isinstance(i, int) else emb[:, bass.ds(at, COLS_IN)]
                    sp.dma_start(emb_sb[:, h, :], of).then_inc(s_emb[h], 16)
            embeddings(0)
            behind = rec_dst_dram[T0 * P:T * P, :].rearrange("(p t) f -> p (t f)", p=P)
            sp.dma_start(behind, zeros[:, 0:(T - T0) * FD]).then_inc(s_zeroed, 16)
            flat = rec_src_dram.rearrange("(p a t) f -> a p (t f)", p=P, a=2)
            for a in range(2):
                sp.dma_start(flat[a], zeros[:, 0:TS // 2 * FS]).then_inc(s_zeroed, 16)
            sp.dma_start(attr, attr_t).then_inc(s_in["attr"], 16)
            sp.dma_start(iw_sb, iw_t).then_inc(s_in["attr"], 16)
            sp.dma_start(ow_sb, ow_t).then_inc(s_in["attr"], 16)
            with sp.Fori(1, STEPS // 8) as i:
                embeddings(i)
            for k in range(2):
                sp.dma_start(wio[:, k, 0:D], w_in[k * P:(k + 1) * P, :]).then_inc(s_in["rows"], 16)
                sp.dma_start(wio[:, k, D:2 * D], w_out[k * P:(k + 1) * P, :]).then_inc(s_in["rows"], 16)
            sp.dma_start(w_even[0:64, :], w00).then_inc(s_in["rows"], 16)
            sp.dma_start(w_even[64:128, :], w11).then_inc(s_in["rows"], 16)
            sp.dma_start(w_odd[0:64, :], w01).then_inc(s_in["rows"], 16)
            sp.dma_start(w_odd[64:128, :], w10).then_inc(s_in["rows"], 16)
            for to, of in ((bn_a[:], gamma), (bn_b[:], beta), (bias_io[:, 0:D], b_in),
                           (bias_io[:, D:2 * D], b_out)):
                sp.dma_start(to, of.to_broadcast([P, of.shape[1]])).then_inc(s_in["rows"], 16)

            sp.wait_ge(s_recs_made, 1)
            sp.wait_ge(s_tables, 1)
            unsorted = sp.value_load(disorder[0:1, 0:1], min_val=0, max_val=1 << 20)
            with sp.If(unsorted > 0):
                for s in s_scat["dst"]:
                    sp.wait_ge(s, 16 * UT // 2 * (T0 // UT))
                sp.sem_inc(s_list, 16)
            with sp.Else():
                sp.dma_start(rec_dst_dram[0:T0 * P, :].rearrange("(p t) f -> p (t f)", p=P),
                             rec_dst.rearrange("p t f -> p (t f)")).then_inc(s_list, 16)
            sp.wait_ge(s_list, 16)
            sp.wait_ge(s_zeroed, 3 * 16)
            start_regs = [sp.alloc_register(f"start{q}") for q in range(2 * R)]
            with sp.Fori(0, T // UT) as i:
                sp.load(start_regs, start_dst[0:1, bass.ds(2 * R * i, 2 * R)])
                for q in range(2 * R):
                    at_row = sp.snap(start_regs[q], min_val=0, max_val=(T - 2) * P)
                    sp.dma_start(srt[:, bass.ds(UT * i + 2 * q, 2), :],
                                 rec_dst_dram[bass.ds(at_row, 2 * P), :].rearrange("(j p) f -> p j f", p=P)
                                 ).then_inc(s_reads, 16)
                sp.wait_ge(s_reads, 16 * 2 * R * (i + 1))
                sp.sem_inc(s_pairs, 1)
            sp.sem_inc(s_pairs, 1)

            sp.wait_ge(loops["l0"]["sums"], R + T // U)
            with sp.Fori(0, NG) as i:
                sp.wait_ge(s_x1, i + 1)
                sp.sem_inc(s_pass, 1)
                sp.dma_start(xin, by_block(x)[:, bass.ds(BG * i, BG), :]).then_inc(s_xin, 16)

            acc_v = acc[:, :].rearrange("p (b f) -> p b f", b=NB)
            with sp.Fori(0, NG) as i:
                g = bass.ds(BG * i, BG)
                sp.wait_ge(nodes["io"]["staged"], i + 1)
                sp.sem_inc(s_pass, 1)
                sp.dma_start(by_block(x1_dram)[:, g, :], acc_v[:, g, 0:D]).then_inc(s_io_dma, 16)
                sp.dma_start(by_block(h_dram)[:, g, :], stage_one).then_inc(s_io_dma, 16)
                sp.wait_ge(nodes["io"]["used"], BG * i + BG + 2)
                sp.sem_inc(s_pass, 1)
                sp.dma_start(by_block(feat_in_dram)[:, g, :], io_stage[:, :, 0:D]).then_inc(s_io_dma, 16)
                sp.dma_start(by_block(feat_out_dram)[:, g, :], io_stage[:, :, D:2 * D]).then_inc(s_io_dma, 16)
                sp.wait_ge(s_io_dma, 64 * i + 64)
                sp.sem_inc(s_pass, 1)
                sp.sem_inc(s_stored, 1)

            for sc in s_scat["src"]:
                sp.wait_ge(sc, 16 * UT // 2 * (T0 // UT))
            sp.wait_ge(s_stored, NG + 1)
            sp.dma_start(msg_flat[:, 0:TS * FS], rec_src_dram.rearrange("(p t) f -> p (t f)", p=P)
                         ).then_inc(s_srt_src, 16)
            sp.wait_ge(s_srt_used, 1)
            for c in range(6):
                w = w_x2i[c * P:(c + 1) * P, :] if c < 4 else w_h2h[(c - 4) * P:(c - 3) * P, :]
                sp.dma_start(wx[:, c, :], w).then_inc(s_wx, 16)
            sp.dma_start(bias_x, b_x2i.to_broadcast([P, 2 * D])).then_inc(s_wx, 16)

            sp.dma_start(h_blk, h_dram[0:P, :]).then_inc(part_in["h"], 16)

            def store_part(rows, i):
                sp.wait_ge(part_in["made"], i + 2)
                sp.sem_inc(s_pass, 1)
                sp.dma_start(gates_dram[rows, :], pre_blk).then_inc(part_in["out"], 16)
            def fetch_x1(b):
                if isinstance(b, int):
                    sp.dma_start(acc[:, D * b:D * b + D], x1_dram[P * b:P * b + P, :]).then_inc(s_x1_in, 16)
                else:
                    sp.dma_start(acc[:, bass.ds(D * b, D)], x1_dram[bass.ds(P * b, P), :]).then_inc(s_x1_in, 16)
            with sp.Fori(0, NB - 1) as i:
                sp.wait_ge(part_in["copied"], i + 2)
                sp.sem_inc(s_pass, 1)
                sp.dma_start(h_blk, h_dram[bass.ds(P * i + P, P), :]).then_inc(part_in["h"], 16)
                fetch_x1(i)
                store_part(bass.ds(P * i, P), i)
            store_part(slice(NP - P, NP), NB - 1)
            fetch_x1(NB - 1)

            sp.wait_ge(part_in["out"], 16 * (NB + 1))
            out_full = out[0:(NB - 1) * P, :].rearrange("(b p) f -> p b f", p=P)
            x1_acc = acc[:, 0:NB * D].rearrange("p (b f) -> p b f", b=NB)

            def fetch(b, j):
                rows = slice(b * P, b * P + P) if isinstance(b, int) else bass.ds(b * P, P)
                sp.dma_start(h_ring[:, j, :], h_dram[rows, :]).then_inc(s_ring[j], 16)
                sp.dma_start(pre_ring[j], gates_dram[rows, :]).then_inc(s_ring[j], 16)
            for j in range(BG):
                fetch(j, j)
            with sp.Fori(0, NG - 1) as i:
                for j in range(BG):
                    sp.wait_ge(s_mixed, BG * i + j + 1 + 2)
                    sp.sem_inc(s_pass, 1)
                    fetch(BG * i + BG + j, j)
                sp.wait_ge(s_out, i + 1)
                sp.sem_inc(s_pass, 1)
                g = bass.ds(BG * i, BG)
                sp.dma_start(out_full[:, g, :], x1_acc[:, g, :]).then_inc(s_out_dma, 16)
            sp.wait_ge(s_out, NG)
            sp.dma_start(out_full[:, BG * (NG - 1):NB - 1, :], x1_acc[:, BG * (NG - 1):NB - 1, :]
                         ).then_inc(s_out_dma, 16)
            rest = N - (NB - 1) * P
            sp.dma_start(out[(NB - 1) * P:N, :], x1_acc[0:rest, NB - 1, :]).then_inc(s_out_dma, 16)
            sp.wait_ge(s_out_dma, 16 * (NG + 1))

        @block.gpsimd
        def _(pool):
            own = Chain(pool, s_pool)
            own.ordered(nc.gpsimd.memset(fc1_bd, 0.0))
            nc.gpsimd.memset(zeros, 0.0).then_inc(s_zero, 1)
            own.ordered(nc.gpsimd.memset(ones[:], 1.0))
            own.ordered(nc.gpsimd.memset(tri[:], 1.0))
            own.ordered(nc.gpsimd.memset(ident[:], 0.0))
            nc.gpsimd.memset(eps[:], EPS)
            own.step(nc.gpsimd.memset(zero[:], 0.0))
            own.ordered(nc.gpsimd.affine_select(out=tri[:], in_=tri[:], compare_op=ALU.is_gt, fill=0.0,
                                                base=0, pattern=[[1, P]], channel_multiplier=-1))
            own.ordered(nc.gpsimd.affine_select(out=ident[:], in_=ident[:], compare_op=ALU.not_equal,
                                                fill=1.0, base=0, pattern=[[1, P]], channel_multiplier=-1))
            nc.gpsimd.iota(iota_row[:], pattern=[[1, P]], base=0, channel_multiplier=0,
                           allow_small_or_imprecise_dtypes=True)
            own.ordered(nc.gpsimd.iota(iota_pair, pattern=[[1, TS]], base=0, channel_multiplier=0,
                                       allow_small_or_imprecise_dtypes=True))
            pool.sem_inc(s_const, 1)

            def wait_here(s, v):
                pool.wait_ge(s, v)
                pool.sem_inc(s_pass, 1)

            nc.gpsimd.memset(rank, 0.0).then_inc(s_pool, 1)
            own.n += 1
            own.settle()
            pool.wait_ge(s_in["weights"], 16 * (PER + 1))

            def weigh(k, q):
                pool.wait_ge(s_hid, k + 1 + 4)
                h = hidden[:, q, :].rearrange("p (t c) -> p t c", c=HID)
                nc.gpsimd.tensor_tensor(h, h, fc2_row[:, :].unsqueeze(1).to_broadcast([P, PER, HID]),
                                        ALU.mult).then_inc(s_weighed, 1)

            def add_places(i, q):
                pool.wait_ge(s_placed, 2 * i + q + 1)
                own.ordered(nc.gpsimd.tensor_tensor(rank, rank, places[q], ALU.add))
                pool.sem_inc(s_ranked, 1)
            with pool.Fori(0, COUNTING // 4) as i:
                for q in range(4):
                    weigh(4 * i + q, q)
            for c in range(SORTING):
                weigh(COUNTING + c, c)
            with pool.Fori(0, SORT_TURNS) as i:
                own.loop(i, 8)
                for j in range(4):
                    for c in range(SORTING):
                        k = SORTING * (j + 1) + c
                        weigh(4 * SORTING * i + (COUNTING + k), k % 4)
                        add_places(4 * i + j, c)
                own.end(SORT_TURNS)
            for k in range(COUNTING + SORTING + 4 * SORTING * SORT_TURNS, STEPS):
                weigh(k, k % 4)
            for q in range(2):
                add_places(4 * SORT_TURNS, q)

            def scatter(chain, key, rec, addr, dram, f):
                half = UT // 2

                def unit(t, h):
                    idx = idx_stage[:, 2 * h:2 * h + 2, :].rearrange("p r u -> p (r u)")
                    records = stage_scatter[:, 2 * h:2 * h + 2, :, :].rearrange("p r u f -> p (r u) f")
                    chain.step(nc.gpsimd.tensor_copy(idx, addr[:, t]))
                    chain.step(nc.gpsimd.tensor_copy(records[:, :, 0:f], rec[:, t, :]))
                    chain.settle()
                    pool.sem_inc(s_pass, 1)
                    for u in range(half):
                        pool.indirect_dma_start(
                            out=dram, out_offset=bass.IndirectOffsetOnAxis(ap=idx[:, u:u + 1], axis=0),
                            in_=records[:, u, 0:f], in_offset=None,
                        ).then_inc(s_scat[key][h], 16)
                for h in range(2):
                    unit(slice(half * h, half * h + half), h)
                with pool.Fori(1, T0 // UT) as i:
                    chain.loop(i - 1, 4)
                    for h in range(2):
                        wait_here(s_scat[key][h], 16 * half * i)
                        unit(bass.ds(UT * i + half * h, half), h)
                    chain.end(T0 // UT - 1)

            pool.wait_ge(s_zeroed, 3 * 16)
            pool.wait_ge(s_tables, 1)
            unsorted = pool.value_load(disorder[0:1, 0:1], min_val=0, max_val=1 << 20)
            pool.sem_inc(s_read, 1)
            with pool.If(unsorted > 0):
                pool.wait_ge(s_addr_dst, 1)
                pool.wait_ge(s_recs_made, 1)
                scatter(Chain(pool, s_pool_branch), "dst", rec_dst, addr_dst, rec_dst_dram, FD)
                for r in range(2):
                    pool.wait_ge(s_scat["dst"][r], 16 * UT // 2 * (T0 // UT))
            with pool.Else():
                pool.sem_inc(s_pass, 1)

            def gathers(k, table, free, tiles=T):
                with pool.Fori(0, tiles // UT) as i:
                    for r in range(R):
                        wait_here(k["idx"], R * i + r + 1)
                        for s in free:
                            wait_here(s, R * i + r + 1)
                        for u in range(U):
                            pool.indirect_dma_start(
                                out=rows_buf[:, U * r + u, :], out_offset=None, in_=table,
                                in_offset=bass.IndirectOffsetOnAxis(ap=idx_stage[:, r, u:u + 1], axis=0),
                            ).then_inc(k["got"][r], 16)

            pool.wait_ge(s_list, 16)
            gathers(loops["l0"], x, (loops["l0"]["sums"],))
            pool.wait_ge(s_addr_src, 1)
            pool.wait_ge(loops["l0"]["idx"], T // U + R)
            scatter(own, "src", rec_src, addr_src, rec_src_dram, FS)
            for r in range(2):
                pool.wait_ge(s_scat["src"][r], 16 * UT // 2 * (T0 // UT))
            pool.sem_inc(s_scattered, 1)
            for name, table in (("in", feat_in_dram), ("out", feat_out_dram)):
                k = loops[name]
                pool.wait_ge(s_stored, NG + 1)
                gathers(k, table, (k["sums"],), TS if name == "out" else T)

            pool.wait_ge(s_x1_in, 16 * NB)
            used = nodes["fin"]["used"]
            with pool.Fori(0, NG) as i:
                for n in range(BG):
                    pool.wait_ge(used, BG * i + n + 1 + 2)
                    x1_blk = acc[:, bass.ds(BG * D * i + D * n, D)]
                    nc.gpsimd.tensor_tensor(x1_blk, x1_blk, gates[:, n % 2, D:2 * D], ALU.add
                                            ).then_inc(s_x1_new, 1)

        @block.scalar
        def _(act):
            act.wait_ge(s_const, 1)
            def silu(k, q):
                act.wait_ge(s_hid_ps, k + 1 + 8)
                act.wait_ge(s_rad, k + 1)
                nc.scalar.activation(hidden[:, q, :], ps[q][:, :], ACT.Silu, scale=1.0 / 10.0 ** 0.5
                                     ).then_inc(s_hid, 1)
            own = Chain(act, s_act)
            act.wait_ge(s_blk, 1)
            with act.Fori(0, SIGN_STEPS) as i:
                own.loop(i, 8)
                for c in range(8):
                    silu(8 * i + c, c % 4)
                    if c < 2:
                        own.settle()
                    else:
                        own.wait(1)
                    b = bass.ds(8 * i + c + 1, 1)
                    own.step(nc.scalar.activation(sign_out[c % 2], blk_dst[:, 0:T0], ACT.Sign,
                                                  bias=half_row[:, b], accum_out=small[:, SIGNS, b]))
                own.end(SIGN_STEPS)
            own.settle()
            act.sem_inc(s_signs, 1)
            with act.Fori(SIGN_STEPS, STEPS // 8) as i:
                for c in range(8):
                    silu(8 * i + c, c % 4)
            act.wait_ge(s_acc_free, 1)
            nc.scalar.activation(acc[:, ACT_ZERO:NB * 2 * D], zero[:, 0:1].to_broadcast([P, NB * 2 * D - ACT_ZERO]),
                                 ACT.Copy).then_inc(s_zero_acc, 1)
            k = loops["l0"]
            with act.Fori(0, T // UT) as i:
                for r in range(R):
                    act.wait_ge(k["got"][r], 16 * U * (i + 1))
                    act.wait_ge(k["sums"], R * i + r + R - 1)
                    for u in range(U - 1):
                        for m in range(3):
                            cm = srt[:, bass.ds(UT * i + U * r + u, 1), SW + 1 + m]
                            nc.scalar.activation(msg[:, 0, r % 2, u, MUL * m:MUL * m + MUL],
                                                 rows_buf[:, U * r + u, 0:MUL], ACT.Copy, scale=cm)
                    act.wait_ge(s_flags, R * i + r + 1)
                    for u in range(U):
                        c0 = srt[:, bass.ds(UT * i + U * r + u, 1), SW]
                        ins = nc.scalar.activation(onehot_c0[:, r % 2, u, :], onehot[:, r % 2, u, :],
                                                   ACT.Copy, scale=c0)
                    ins.then_inc(k["scaled"], 1)

            def copy_turned(st, i, j, width):
                act.wait_ge(st["turns"], BG * i + j + 1)
                act.wait_ge(st["sums"], BG * i + j + before(j))
                to = turned[j % 2]
                nc.scalar.copy(to[:, 0:width], ps[j % 2][:, 0:width]).then_inc(st["copied"], 1)

            def deviations(st, i):
                act.wait_ge(st["var"], i + 1)
                nc.scalar.activation(rstd[:, :], mv[:, :, 1:2].rearrange("p b o -> p (b o)"), ACT.Sqrt,
                                     bias=eps[:, 0:1]).then_inc(st["sd"], 1)

            with act.Fori(0, NG) as i:
                for j in range(BG):
                    copy_turned(nodes["l0"], i, j, 512)
                deviations(nodes["l0"], i)
            act.wait_ge(s_bnv, 1)
            nc.scalar.activation(bn_sd, bn_var, ACT.Sqrt, bias=eps[:, 0:1]).then_inc(s_bnsd, 1)
            with act.Fori(0, NG) as i:
                for j in range(BG):
                    copy_turned(nodes["io"], i, j, 256)
            act.wait_ge(loops["in"]["added"], 2 * LAG + PAIRS)
            act.wait_ge(s_srt_used, 1)
            with act.Fori(0, NB) as i:
                nc.scalar.copy(a_blk, acc[:, bass.ds(D * i, D)]).then_inc(part_in["staged"], 1)
                act.wait_ge(part_in["turns"], i + 1)
                act.wait_ge(part_in["sums"], i + 1)
                nc.scalar.copy(turned[1][:, 0:2 * D], ps[4][:, :]).then_inc(part_in["copied"], 1)
            st = nodes["fin"]

            def gates_of(i, first):
                for j in range(BG + 1):
                    if j == 2 and not first:
                        deviations(st, i - 1)
                    if j < BG:
                        copy_turned(st, i, j, 256)
                    if j >= 1:
                        n = j - 1
                        act.wait_ge(s_pre, BG * i + n + 1)
                        act.wait_ge(s_mixed, BG * i + n + before(n))
                        nc.scalar.activation(gates[:, n % 2, 0:D], ps[4 + n % 2][:, 0:D], ACT.Sigmoid)
                        nc.scalar.activation(gates[:, n % 2, D:2 * D], ps[4 + n % 2][:, D:2 * D],
                                             ACT.Tanh).then_inc(st["used"], 1)
            gates_of(0, True)
            with act.Fori(1, NG) as i:
                gates_of(i, False)
            deviations(st, NG - 1)

        @block.tensor
        def _(pe):
            pe.wait_ge(s_in["weights"], 16 * (PER + 1))
            pe.sem_inc(s_hid_ps, 8)
            pe.sem_inc(s_hid, 4)

            def radial_step(i):
                for h in range(2):
                    pe.wait_ge(s_emb[h], 16 * (i + 1))
                    for c in range(4):
                        pe.wait_ge(s_hid, 8 * i + 4 * h + c + 1)
                        pe.matmul(ps[c][:, :], emb_sb[:, h, P * c:P * c + P], fc1_bd,
                                  start=True, stop=True).then_inc(s_hid_ps, 1)

            def sum_counts(n):
                pe.matmul(ps[6][:, 64 * n:64 * n + NB], tri[:, :], small[:, CNT + n, 0:NB], start=True, stop=True)
                return pe.matmul(ps[7][:, 64 * n:64 * n + NB], ones[:, :], small[:, CNT + n, 0:NB],
                                 start=True, stop=True)
            with pe.Fori(0, SRC_STEP) as i:
                radial_step(i)
            pe.wait_ge(s_const, 1)
            pe.wait_ge(s_cnt["src"], 1)
            sum_counts(1).then_inc(s_cnt_ps["src"], 1)
            with pe.Fori(SRC_STEP, STEPS // 8) as i:
                radial_step(i)
            pe.wait_ge(s_cnt["dst"], 1)
            sum_counts(0)
            pe.matmul(ps[7][:, 128:129], ones[:, :], small[:, MISC, 0:1], start=True, stop=True
                      ).then_inc(s_cnt_ps["dst"], 1)
            pe.wait_ge(s_tend, 1)
            for c, row in enumerate((TEND, TEND + 1, PADS)):
                ins = pe.matmul(ps[6][0:NB, c:c + 1], small[0:1, row, 0:NB], ones[0:1, 0:1], start=True, stop=True)
            ins.then_inc(s_tend_ps, 1)
            pe.wait_ge(s_past, 1)
            pe.matmul(ps[6][:, 0:PAIRS], ones[0:NB, :], past[0][0:NB, :], start=True, stop=True)
            for h in range(2):
                pe.matmul(ps[5 + 2 * h][:, 0:TS // 2], ones[0:NB, :], past[1][0:NB, TS // 2 * h:TS // 2 * (h + 1)],
                          start=True, stop=True)
            pe.matmul(ps[4][0:1, 0:PAIRS], small[0:NB, COLS, 2:3], past[0][0:NB, :], start=True, stop=True
                      ).then_inc(s_past_ps, 1)
            pe.wait_ge(s_tables, 1)

            def edge_sums(k, ready, products, kind, between=None):
                tiles = 1 if kind == "out" else 2

                def round_of(i, between):
                    for r in range(R):
                        if r in between:
                            between[r](i)
                        for s, v in ready(i, r):
                            pe.wait_ge(s, v)
                        pe.wait_ge(k["added"], 4 * (R * i + r) + 4 if kind == "out" else 2 * (R * i + r) + 2)
                        for u in range(U):
                            parts = products(r, u)
                            for c, (hot, rows, at, n) in enumerate(parts):
                                bank, first = place_of((U * r + u) // tiles, kind)
                                ins = pe.matmul(ps[bank][:, first + at:first + at + n], hot, rows,
                                                start=u % tiles == 0 and c == 0,
                                                stop=u % tiles == tiles - 1 and c == len(parts) - 1,
                                                skip_group_check=True)
                        ins.then_inc(k["sums"], 1)
                if between:
                    with pe.Fori(0, NB) as i:
                        round_of(i, between)
                with pe.Fori(NB if between else 0, (TS if kind == "out" else T) // UT) as i:
                    round_of(i, {})

            k0 = loops["l0"]
            edge_sums(k0, lambda i, r: ((k0["hot"], R * i + r + 2), (k0["scaled"], R * i + r + 1)),
                      lambda r, u: ((onehot_c0[:, r % 2, u, :], rows_buf[:, U * r + u, :], 0, D),
                                    (onehot[:, r % 2, u, :], msg[:, 0, r % 2, u, :], D, D)), "l0")

            def products(st, turn, product, ready):
                with pe.Fori(0, NG) as i:
                    for s, per in ready:
                        pe.wait_ge(s, per * (i + 1))
                    for j in range(BG + 1):
                        if j < BG:
                            pe.wait_ge(st["copied"], BG * i + j + before(j))
                            turn(j).then_inc(st["turns"], 1)
                        if j >= 1:
                            n = j - 1
                            pe.wait_ge(st["copied"], BG * i + n + 1 + 2)
                            pe.wait_ge(st["used"], BG * i + n + before(n))
                            product(n).then_inc(st["sums"], 1)

            def turn(parts, first_bank):
                for c, of in enumerate(parts):
                    ins = pe.transpose(ps[first_bank][:, P * c:P * c + P], of, ident[:, :])
                return ins

            def halves(v):
                return [v[:, 0:P], v[:, P:D]]

            def weights0(j):
                for c in range(4):
                    ins = pe.matmul(ps[4 + j % 2][:, MUL * c:MUL * c + MUL], turned[j % 2][:, P * c:P * c + P],
                                    (w_odd if c else w_even)[:, :], start=True, stop=True)
                return ins

            def weights(parts):
                def product(j):
                    for c, w in enumerate(parts):
                        ins = pe.matmul(ps[4 + j % 2][:, :], turned[j % 2][:, P * c:P * c + P], w,
                                        start=c == 0, stop=c == len(parts) - 1)
                    return ins
                return product

            pe.wait_ge(s_wconst, 1)
            products(nodes["l0"], lambda j: turn([stage[:, j, P * c:P * c + P] for c in range(4)], j % 2),
                     weights0, ((nodes["l0"]["staged"], 1),))

            acc_v = acc[:, :].rearrange("p (b f) -> p b f", b=NB)
            pe.wait_ge(s_x1, NG + 1)
            pe.matmul(ps[6][:, 0:D], ones[:, :], acc_v[:, 0, 0:D], start=True, stop=False)
            with pe.Fori(1, NB - 1) as b:
                pe.matmul(ps[6][:, 0:D], ones[:, :], acc_v[:, bass.ds(b, 1), 0:D].rearrange("p a f -> p (a f)"),
                          start=False, stop=False)
            pe.matmul(ps[6][:, 0:D], ones[:, :], acc_v[:, NB - 1, 0:D], start=False, stop=True
                      ).then_inc(s_sum_ps, 1)

            def squares(first, last):
                for j in range(BG):
                    ins = pe.matmul(ps[7][:, 0:D], ones[:, :], stage_one[:, j, :],
                                    start=first and j == 0, stop=last and j == BG - 1)
                ins.then_inc(s_sq_ps, 1)
            pe.wait_ge(s_sq, 1)
            squares(True, False)
            with pe.Fori(1, NG - 1) as i:
                pe.wait_ge(s_sq, i + 1)
                squares(False, False)
            pe.wait_ge(s_sq, NG)
            squares(False, True)

            products(nodes["io"], lambda j: turn(halves(stage_one[:, j, :]), j % 2),
                     weights([wio[:, 0, :], wio[:, 1, :]]), ((nodes["io"]["staged"], 1),))

            def turn_part(i):
                pe.wait_ge(part_in["h"], 16 * (i + 1))
                pe.wait_ge(part_in["staged"], i + 1)
                pe.wait_ge(part_in["copied"], i + 1)
                for c in range(2):
                    pe.transpose(ps[4][:, P * c:P * c + P], a_blk[:, P * c:P * c + P], ident[:, :])
                for c in range(2):
                    ins = pe.transpose(ps[4][:, D + P * c:D + P * c + P], h_blk[:, P * c:P * c + P], ident[:, :])
                ins.then_inc(part_in["turns"], 1)

            def multiply_part(terms):
                def run(i):
                    if 0 in terms:
                        pe.wait_ge(s_wx, 7 * 16)
                        pe.wait_ge(part_in["copied"], i + 2)
                        pe.wait_ge(part_in["made"], i + 1)
                    for c in terms:
                        ins = pe.matmul(ps[5][:, :], turned[1][:, P * c:P * c + P], wx[:, (0, 1, 4, 5)[c], :],
                                        start=c == 0, stop=c == 3, skip_group_check=True)
                    if 3 in terms:
                        ins.then_inc(part_in["sums"], 1)
                return run

            for name in ("in", "out"):
                k1 = loops[name]
                edge_sums(k1, lambda i, r: ((k1["hot"], R * i + r + 1), (k1["got"][r], 16 * U * (i + 1))),
                          lambda r, u: ((onehot[:, r % 2, u, :], rows_buf[:, U * r + u, :], 0, D),), name,
                          {0: turn_part, 1: multiply_part((0,)), 2: multiply_part((1, 2)), 3: multiply_part((3,))} if name == "out" else None)

            products(nodes["fin"], lambda j: turn(halves(stage_one[:, j, :]), j % 2),
                     weights([wx[:, 2, :], wx[:, 3, :]]), ((nodes["fin"]["staged"], 1),))

        @block.vector
        def _(dve):
            own = Chain(dve, s_dve)
            V = nc.vector
            for k in loops.values():
                dve.sem_inc(k["added"], LAG)
                dve.sem_inc(k["sums"], R)
            for st in nodes.values():
                for name in ("copied", "sums", "used"):
                    dve.sem_inc(st[name], 2)
            dve.sem_inc(s_mixed, 2)
            dve.sem_inc(s_rad, 4)
            dve.sem_inc(loops["l0"]["hot"], 1)
            own.step(V.memset(block_dst[:, :], 0))
            own.step(V.memset(block_src[:, :], 0))
            own.step(V.memset(srt[:, T:T + UT, :], 0.0))
            own.step(V.memset(base_row[:, PAIRS:PAIRS + 2 * R], 0.0))
            own.step(V.memset(small[:, :, :], 0.0))
            own.step(V.memset(rec_dst[:, :, FD - 1:FD], 0.0))
            own.ordered(V.memset(rec_src[:, :, FS - 1:FS], 0.0))
            dve.sem_inc(s_ranked, 2)
            dve.wait_ge(s_const, 1)

            dve.wait_ge(s_in["dst"], 16)
            dve.wait_ge(s_in["src"], 16)
            dst, src = key_dst[:, 0:T0], key_src
            shifted = flags[0].bitcast(I32)
            own.ordered(V.tensor_scalar(key_dst_blk, key_dst, 7, None, ALU.arith_shift_right))
            own.ordered(V.tensor_copy(blk_dst, key_dst_blk))
            own.step(V.tensor_scalar(half_row[:, :], iota_row[:, 0:64], -1.0, 0.5, ALU.mult, ALU.add))
            own.step(V.memset(small[:, SIGNS, 0:1], float(T0)))
            own.ordered(V.memset(small[:, SIGNS, NB:NB + 1], -float(T0)))
            own.ordered(V.tensor_scalar(tmp_i, src, 7, None, ALU.arith_shift_right))
            own.ordered(V.tensor_copy(blk_src, tmp_i))
            dve.sem_inc(s_blk, 1)
            own.ordered(V.tensor_scalar(shifted, src, P - 1, None, ALU.bitwise_and))
            own.ordered(V.tensor_copy(rec_src[:, :, SLOC], shifted))
            own.step(V.tensor_copy(rec_dst[:, :, SLOC], dst))
            own.ordered(V.tensor_tensor(flags[0], blk_dst[:, 0:T0], blk_dst[:, 1:T0 + 1], ALU.is_gt))
            own.step(V.tensor_reduce(small[:, MISC, 0:1], flags[0], mybir.AxisListType.X, ALU.add))
            own.settle()

            def radial(k, q):
                dve.wait_ge(s_weighed, k + 1)
                to = rad[:, PER * k:PER * k + PER] if isinstance(k, int) else rad[:, bass.ds(PER * k, PER)]
                V.tensor_reduce(to, hidden[:, q, :].rearrange("p (t c) -> p t c", c=HID),
                                mybir.AxisListType.X, ALU.add).then_inc(s_rad, 1)

            def count_src(b, q):
                at = slice(b, b + 1) if isinstance(b, int) else bass.ds(b, 1)
                own.step(V.tensor_scalar(places[q], blk_src, iota_row[:, at], None, ALU.is_equal,
                                         ALU.add, accum_out=small[:, CNT + 1, at]))
            with dve.Fori(0, COUNTING // 4) as i:
                own.loop(i, 4)
                for q in range(4):
                    own.wait(1)
                    count_src(4 * i + q, q % 2)
                    radial(4 * i + q, q)
                own.end(COUNTING // 4)
            own.settle()
            count_src(NB - 1, 0)
            own.settle()
            dve.sem_inc(s_cnt["src"], 1)
            ints = small[:, INTS:INTS + 2, 0:NB].bitcast(I32)

            def block_ends(n):
                bits = 7 if n else 8
                count = ps[7][:, 64 * n:64 * n + NB]
                pairs, tend, tstart = (small[:, q + n, 0:NB] for q in (PAIRN, TEND, TSTART))
                own.ordered(V.tensor_scalar(ints[:, 0, :], count, float((1 << bits) - 1), None, ALU.add))
                own.ordered(V.tensor_scalar(ints[:, 1, :], ints[:, 0, :], bits, None, ALU.arith_shift_right))
                own.ordered(V.tensor_copy(pairs, ints[:, 1, :]))
                own.ordered(V.tensor_tensor_scan(tend, pairs, pairs, 0.0, ALU.add, ALU.max))
                own.ordered(V.tensor_tensor(tstart, tend, pairs, ALU.subtract))
            dve.wait_ge(s_cnt_ps["src"], 1)
            block_ends(1)
            own.ordered(V.scalar_tensor_tensor(out=small[:, BASE + 1, 0:NB], in0=small[:, TSTART + 1, 0:NB],
                                               scalar=float(P), in1=ps[6][:, 64:64 + NB], op0=ALU.mult, op1=ALU.add))
            def block_of(n):
                return slice(n, n + 1) if isinstance(n, int) else bass.ds(n, 1)

            def sort_two(i, k):
                for q in range(2):
                    own.step(V.tensor_scalar(flags[q], blk_src, iota_row[:, block_of(2 * i + q)], None,
                                             ALU.is_equal))
                k(0)
                for q in range(2):
                    own.wait(1)
                    own.step(V.tensor_tensor_scan(counts[q], flags[q], flags[q],
                                                  small[:, BASE + 1, block_of(2 * i + q)], ALU.add, ALU.max))
                k(1)
                own.settle()
                for q in range(2):
                    dve.wait_ge(s_ranked, 2 * i + q + 1)
                    V.tensor_tensor(places[q], flags[q], counts[q], ALU.mult).then_inc(s_placed, 1)
                dve.wait_ge(s_placed, 2 * i + 2)
            with dve.Fori(0, SORT_TURNS) as i:
                own.loop(i, 4 * 4)
                for j in range(4):
                    sort_two(4 * i + j, lambda c: radial(4 * SORTING * i + (COUNTING + SORTING * j + c),
                                                         (SORTING * j + c) % 4))
                own.end(SORT_TURNS)
            first = COUNTING + 4 * SORTING * SORT_TURNS
            sort_two(4 * SORT_TURNS, lambda c: radial(first + c, (first + c) % 4))
            dve.wait_ge(s_signs, 1)
            own.ordered(V.tensor_tensor(small[:, CNT, 0:NB], small[:, SIGNS, 0:NB], small[:, SIGNS, 1:NB + 1],
                                        ALU.subtract))
            own.ordered(V.tensor_scalar(small[:, CNT, 0:NB], small[:, CNT, 0:NB], 0.5, None, ALU.mult))
            dve.sem_inc(s_cnt["dst"], 1)
            dve.wait_ge(s_cnt_ps["dst"], 1)
            own.step(V.tensor_copy(disorder, ps[7][:, 128:129]))
            block_ends(0)
            lst, total = small[:, BASE, 0:NB], small[:, TSTART, 0:NB]
            own.ordered(V.scalar_tensor_tensor(out=small[:, PADS, 0:NB], in0=small[:, PAIRN, 0:NB], scalar=2.0 * P,
                                               in1=ps[7][:, 0:NB], op0=ALU.mult, op1=ALU.subtract))
            own.ordered(V.tensor_copy(total, ps[7][:, 0:NB]))
            own.ordered(V.tensor_tensor_scan(lst, total, total, 0.0, ALU.add, ALU.max))
            own.ordered(V.tensor_tensor(lst, lst, total, ALU.subtract))
            own.ordered(V.tensor_tensor(lst, lst, ps[6][:, 0:NB], ALU.add))
            dve.sem_inc(s_tend, 1)
            dve.wait_ge(s_tend_ps, 1)
            own.ordered(V.tensor_copy(small[0:NB, COLS, 0:3], ps[6][0:NB, 0:3]))
            for n in range(2):
                own.step(V.tensor_scalar(past[n][0:NB, :], iota_pair[0:NB, 0:TS if n else PAIRS], small[0:NB, COLS, n:n + 1], None,
                                         ALU.is_ge))
            own.settle()
            dve.sem_inc(s_past, 1)
            dve.wait_ge(s_past_ps, 1)
            own.step(V.tensor_scalar(block_dst[0:1, LAG:LAG + PAIRS], ps[6][0:1, 0:PAIRS], float(NB - 1), None, ALU.min))
            for h in range(2):
                own.step(V.tensor_scalar(block_src[0:1, LAG + TS // 2 * h:LAG + TS // 2 * (h + 1)],
                                         ps[5 + 2 * h][0:1, 0:TS // 2], float(NB - 1), None, ALU.min))
            own.step(V.tensor_scalar(base_row[:, 0:PAIRS], ps[6][:, 0:PAIRS], float(NB - 1), -float(P),
                                     ALU.min, ALU.mult))
            own.ordered(V.scalar_tensor_tensor(out=start_dst[0:1, :], in0=iota_pair[0:1, 0:PAIRS], scalar=2.0 * P,
                                               in1=ps[4][0:1, 0:PAIRS], op0=ALU.mult, op1=ALU.subtract))
            dve.sem_inc(s_tables, 1)
            for k in range(first + SORTING, STEPS):
                radial(k, k % 4)

            def write_addresses(chain):
                chain.ordered(V.tensor_scalar(tmp_i, rank, -1.0, None, ALU.add))
                chain.ordered(V.tensor_scalar(shifted, tmp_i, 7, None, ALU.arith_shift_right))
                chain.ordered(V.tensor_copy(tmp_f, shifted))
                chain.ordered(V.tensor_scalar(shifted, tmp_i, P - 1, None, ALU.bitwise_and))
                chain.ordered(V.tensor_copy(tmp_g, shifted))
                chain.ordered(V.scalar_tensor_tensor(out=addr_src[:, :], in0=tmp_g, scalar=float(TS), in1=tmp_f,
                                                     op0=ALU.mult, op1=ALU.add))
            dve.wait_ge(s_in["attr"], 48)
            dve.wait_ge(s_rad, 4 + STEPS)
            own.step(V.tensor_copy(rec_dst[:, :, DIN].bitcast(I32), src))
            own.step(V.tensor_copy(rec_src[:, :, DIN].bitcast(I32), dst))
            for c in range(4):
                own.step(V.scalar_tensor_tensor(out=rec_dst[:, :, SW + c], in0=attr[:, :, c],
                                                scalar=SILU_NORM / 8.0, in1=rad, op0=ALU.mult, op1=ALU.mult))
            own.step(V.tensor_copy(rec_dst[:, :, WIN], iw_sb))
            own.ordered(V.tensor_copy(rec_src[:, :, SW], ow_sb))
            dve.sem_inc(s_recs_made, 1)
            dve.wait_ge(s_ranked, 2 + NB + 1)
            write_addresses(own)
            dve.sem_inc(s_addr_src, 1)

            unsorted = dve.value_load(disorder[0:1, 0:1], min_val=0, max_val=1 << 20)
            with dve.If(unsorted > 0):
                chain = Chain(dve, s_dve_branch)
                chain.ordered(V.memset(rank, 0.0))
                with dve.Fori(0, NB) as b:
                    chain.loop(b, 4)
                    chain.ordered(V.tensor_scalar(flags[0], blk_dst[:, 0:T0], iota_row[:, bass.ds(b, 1)], None,
                                                  ALU.is_equal))
                    chain.ordered(V.tensor_tensor_scan(counts[0], flags[0], flags[0],
                                                       small[:, BASE, bass.ds(b, 1)], ALU.add, ALU.max))
                    chain.ordered(V.tensor_tensor(places[0], flags[0], counts[0], ALU.mult))
                    chain.ordered(V.tensor_tensor(rank, rank, places[0], ALU.add))
                    chain.end(NB)
                chain.ordered(V.tensor_scalar(addr_dst, rank, -1.0, None, ALU.add))
                dve.sem_inc(s_addr_dst, 1)
            with dve.Else():
                dve.sem_inc(s_pass, 1)
            dve.wait_ge(s_read, 1)
            dve.wait_ge(s_list, 16)
            dve.sem_inc(s_acc_free, 1)

            dve.wait_ge(s_in["rows"], 16 * 12)
            alpha = (2.0 * MUL) ** -0.5 / 4.0
            own.step(V.tensor_scalar(w_odd[:, :], w_odd[:, :], alpha, None, ALU.mult))
            own.step(V.tensor_scalar(w_even[0:64, :], w_even[0:64, :], alpha, None, ALU.mult))
            own.ordered(V.tensor_scalar(w_even[64:128, :], w_even[64:128, :], alpha * 3.0 ** -0.5, None, ALU.mult))
            dve.sem_inc(s_wconst, 1)

            def edge_loop(k, rec, table, width, offset, first, second, per, between=None):
                fresh = k is loops["l0"]

                def in_block(i):
                    loc = srt[:, bass.ds(UT * i, UT), SLOC].rearrange("p (q j) -> p q j", j=2)
                    minus = base_row[:, bass.ds(2 * R * i, 2 * R)].unsqueeze(2).to_broadcast([P, 2 * R, 2])
                    own.step(V.tensor_tensor(loc, loc, minus, ALU.add))
                if fresh:
                    dve.wait_ge(s_pairs, 1)
                    in_block(0)
                index = rec[:, :, DIN].bitcast(I32)
                if k is loops["in"]:
                    own.ordered(V.memset(acc[:, :], 0.0))
                    dve.wait_ge(s_scattered, 1)
                for r in range(R):
                    V.tensor_copy(idx_stage[:, r, :], index[:, U * r:U * r + U]).then_inc(k["idx"], 1)

                def load_blocks(place, n):
                    regs = block_regs[:n]
                    dve.load(regs, table[0:1, bass.ds(place, n)])
                    return [dve.snap(r, min_val=0, max_val=NB - 1) for r in regs]

                by_src = k is loops["out"]
                kind = "l0" if fresh else "out" if by_src else "in"
                sums, late = (TS, 1) if by_src else (PAIRS, 2)
                of_unit = 4 if by_src else 2
                rounds = (TS if by_src else T) // UT

                def sums_of(pair):
                    bank, first = place_of(pair, kind)
                    return ps[bank][:, first:first + width]

                def add(blk, pair, count):
                    to = acc[:, bass.ds(blk * width + offset, width)]
                    dve.wait_ge(k["added"], count)
                    V.tensor_tensor(to, to, sums_of(pair), ALU.add).then_inc(k["added"], 1)

                for q in range(LAG):
                    own.step(V.memset(sums_of(R * of_unit - LAG + q), 0.0))
                own.settle()
                if fresh:
                    own.ordered(V.memset(acc[:, 0:ACT_ZERO], 0.0))
                    dve.wait_ge(s_zero_acc, 1)
                def round_of(i, base, trips, between):
                    own.loop(i - base if base else i, R * per + fresh + (1 if between else 0))
                    own.settle()
                    blocks = load_blocks(of_unit * R * i, of_unit * R)
                    if fresh:
                        dve.wait_ge(s_pairs, i + 2)
                        in_block(i + 1)
                    for r in range(R):
                        dve.wait_ge(k["sums"], R * i + r + R - 1)
                        first(i, r)
                        dve.wait_ge(k["got"][r], 16 * U * (i + 1))
                        V.tensor_copy(idx_stage[:, r, :], index[:, bass.ds(UT * i + UT + U * r, U)]
                                      ).then_inc(k["idx"], 1)
                        if late == 1:
                            dve.wait_ge(k["sums"], R * i + r + R)
                        for q in range(of_unit):
                            if q < 2:
                                second[q](i, r)
                            n = of_unit * r + q
                            add(blocks[n], (n - of_unit * late) % (of_unit * R), LAG + of_unit * R * i + n)
                        if between and r in between:
                            between[r](i)
                    own.end(trips)
                start = NB if between else 0
                if between:
                    with dve.Fori(0, NB) as i:
                        round_of(i, 0, NB, between)
                with dve.Fori(start, rounds) as i:
                    round_of(i, start, rounds - start, None)
                dve.wait_ge(k["sums"], R + R * rounds)
                last = load_blocks(sums, LAG)
                for q in range(LAG):
                    add(last[q], R * of_unit - LAG + q, LAG + sums + q)
                dve.wait_ge(k["added"], 2 * LAG + sums)

            block_regs = [dve.alloc_register(f"block{q}") for q in range(4 * R)]

            def unit_of(i, r):
                return rows_buf[:, U * r:U * r + U, :], bass.ds(UT * i + U * r, U)

            def flags0(i, r):
                g, t = unit_of(i, r)
                V.tensor_tensor(onehot[:, r % 2, :, :], srt[:, t, SLOC:SLOC + 1].to_broadcast([P, U, P]),
                                iota_row[:, :].unsqueeze(1).to_broadcast([P, U, P]), ALU.is_equal
                                ).then_inc(s_flags, 1)

            def products0(i, r):
                g, t = unit_of(i, r)
                s1 = g[:, :, MUL:D].rearrange("p u (i m) -> p u i m", m=3)
                dve.wait_ge(loops["l0"]["hot"], R * i + r + 1)
                own.step(V.tensor_tensor(prod[:, :, :, :], s1,
                                         srt[:, t, SW + 1:SW + 4].unsqueeze(2).to_broadcast([P, U, MUL, 3]),
                                         ALU.mult))

            def messages0(i, r):
                own.settle()
                last = srt[:, bass.ds(UT * i + U * r + U - 1, 1), SW + 1:SW + 4].rearrange("p a m -> p (a m)")
                V.tensor_tensor(msg[:, 0, r % 2, U - 1, 0:3 * MUL].rearrange("p (m i) -> p m i", m=3),
                                rows_buf[:, U * r + U - 1, 0:MUL].unsqueeze(1).to_broadcast([P, 3, MUL]),
                                last.unsqueeze(2).to_broadcast([P, 3, MUL]), ALU.mult)
                V.tensor_reduce(msg[:, 0, r % 2, :, 3 * MUL:D], prod[:, :, :, :], mybir.AxisListType.X, ALU.add
                                ).then_inc(loops["l0"]["hot"], 1)

            edge_loop(loops["l0"], srt, block_dst, 2 * D, 0, flags0, (products0, messages0), 1)

            acc_v = acc[:, :].rearrange("p (b f) -> p b f", b=NB)
            dve.sem_inc(s_x1, 1)

            def normalise(st, i, to):
                for j in range(BG):
                    own.step(V.bn_stats(stats[:, j, :], to[j]))
                own.settle()
                dve.sem_inc(s_pass, 1)
                for j in range(BG):
                    own.step(V.bn_aggr(mv[:, j, :], stats[:, j, :]))
                own.settle()
                dve.sem_inc(st["var"], 1)
                dve.wait_ge(st["sd"], i + 1)
                own.ordered(V.reciprocal(rstd[:, :], rstd[:, :]))

            st = nodes["l0"]
            with dve.Fori(0, NG) as i:
                own.loop(i, 8 + 2 * BG + 2 * BG + 1 + BG)
                group = bass.ds(BG * i, BG)
                own.step(V.tensor_copy(stage[:, :, 0:MUL], acc_v[:, group, 0:MUL]))
                own.step(V.tensor_copy(stage[:, :, MUL:P], acc_v[:, group, 7 * MUL:8 * MUL]))
                for m in range(3):
                    to = stage[:, :, P * (m + 1):P * (m + 2)]
                    own.step(V.tensor_copy(to[:, :, 0:MUL], acc_v[:, group, D + MUL * m:D + MUL * (m + 1)]))
                    own.step(V.tensor_copy(to[:, :, MUL:P], acc_v[:, group, MUL:D].rearrange(
                        "p b (i m) -> p b i m", m=3)[:, :, :, m]))
                own.settle()
                dve.sem_inc(st["staged"], 1)
                dve.wait_ge(s_xin, 16 * (i + 1))
                for j in range(BG):
                    dve.wait_ge(st["sums"], BG * i + j + 1 + 2)
                    y = ps[4 + j % 2]
                    own.step(V.tensor_tensor(xin[:, j, 0:MUL], xin[:, j, 0:MUL], y[:, 0:MUL], ALU.add))
                    v = xin[:, j, MUL:D].rearrange("p (o m) -> p m o", m=3)
                    own.ordered(V.tensor_tensor(v, v, y[:, MUL:D].rearrange("p (m o) -> p m o", m=3), ALU.add))
                    dve.sem_inc(st["used"], 1)
                normalise(st, i, [xin[:, j, :] for j in range(BG)])
                for j in range(BG):
                    own.step(V.tensor_scalar(acc_v[:, bass.ds(BG * i + j, 1), 0:D].rearrange("p a f -> p (a f)"),
                                             xin[:, j, :], mv[:, j, 0:1], rstd[:, j:j + 1], ALU.subtract, ALU.mult))
                own.settle()
                dve.sem_inc(s_x1, 1)
                own.end(NG)

            dve.wait_ge(s_sum_ps, 1)
            own.ordered(V.tensor_scalar(mean_row[:, :], ps[6][:, 0:D], 1.0 / N, None, ALU.mult))

            def squares(i):
                x1 = acc_v[:, bass.ds(BG * i, BG), 0:D] if not isinstance(i, int) else acc_v[:, 0:BG, 0:D]
                own.ordered(V.tensor_tensor(stage_one, x1, mean_row[:, :].unsqueeze(1).to_broadcast([P, BG, D]),
                                            ALU.subtract))
                own.ordered(V.tensor_tensor(stage_one, stage_one, stage_one, ALU.mult))
                dve.sem_inc(s_sq, 1)
            squares(0)
            with dve.Fori(1, NG) as i:
                dve.wait_ge(s_sq_ps, i)
                own.loop(i - 1, 2)
                squares(i)
                own.end(NG - 1)
            dve.wait_ge(s_sq_ps, NG)
            own.ordered(V.tensor_tensor(bn_sd, mean_row[:, :], mean_row[:, :], ALU.mult))
            own.ordered(V.scalar_tensor_tensor(out=bn_var, in0=bn_sd, scalar=-float(NP - N), in1=ps[7][:, 0:D],
                                               op0=ALU.mult, op1=ALU.add))
            own.ordered(V.tensor_scalar(bn_var, bn_var, 1.0 / N, None, ALU.mult))
            dve.sem_inc(s_bnv, 1)
            dve.wait_ge(s_bnsd, 1)
            own.ordered(V.reciprocal(bn_sd, bn_sd))
            own.ordered(V.tensor_tensor(bn_a[:, :], bn_a[:, :], bn_sd, ALU.mult))
            own.ordered(V.tensor_tensor(bn_sd, mean_row[:, :], bn_a[:, :], ALU.mult))
            own.ordered(V.tensor_tensor(bn_b[:, :], bn_b[:, :], bn_sd, ALU.subtract))

            st = nodes["io"]
            dve.sem_inc(s_stored, 1)
            with dve.Fori(0, NG) as i:
                own.loop(i, 2 + BG)
                x1 = acc_v[:, bass.ds(BG * i, BG), 0:D]
                dve.wait_ge(s_stored, i + 1)
                own.ordered(V.tensor_tensor(stage_one, x1, bn_a[:, :].unsqueeze(1).to_broadcast([P, BG, D]), ALU.mult))
                own.ordered(V.tensor_tensor(stage_one, stage_one, bn_b[:, :].unsqueeze(1).to_broadcast([P, BG, D]),
                                            ALU.add))
                dve.sem_inc(st["staged"], 1)
                for j in range(BG):
                    dve.wait_ge(st["sums"], BG * i + j + 1 + 2)
                    own.ordered(V.tensor_tensor(io_stage[:, j, :], ps[4 + j % 2][:, :], bias_io[:, :], ALU.add))
                    dve.sem_inc(st["used"], 1)
                own.end(NG)
            dve.wait_ge(s_stored, NG + 1)

            def layer1(name, rec, table, offset, w, between=None):
                def weighted(i, r):
                    for u in range(U):
                        t = bass.ds(UT * i + U * r + u, 1)
                        ins = V.tensor_scalar(onehot[:, r % 2, u, :], iota_row[:, :], rec[:, t, SLOC],
                                              rec[:, t, w], ALU.is_equal, ALU.mult)
                    ins.then_inc(loops[name]["hot"], 1)

                def nothing(i, r):
                    pass
                edge_loop(loops[name], rec, table, D, offset, weighted, (nothing, nothing), 0, between)
            layer1("in", srt, block_dst, 0, WIN)
            dve.sem_inc(s_srt_used, 1)
            own.ordered(V.memset(srt_src[:, TS:TS + UT, :], 0.0))
            dve.wait_ge(s_srt_src, 16)

            def part_made(i):
                dve.wait_ge(part_in["sums"], i + 2)
                dve.wait_ge(part_in["out"], 16 * (i + 1))
                own.ordered(V.tensor_tensor(pre_blk, ps[5][:, :], bias_x, ALU.add))
                dve.sem_inc(part_in["made"], 1)
            dve.sem_inc(part_in["copied"], 1)
            dve.sem_inc(part_in["sums"], 1)
            dve.sem_inc(part_in["made"], 1)
            dve.sem_inc(part_in["out"], 16)
            layer1("out", srt_src, block_src, NB * D, SW, {3: part_made})

            st = nodes["fin"]
            dve.wait_ge(s_x1_in, 16 * NB)

            def stage_out(i):
                at = NB * D + BG * D * i
                of = acc[:, at:at + BG * D] if isinstance(i, int) else acc[:, bass.ds(at, BG * D)]
                own.ordered(V.tensor_copy(msg_flat[:, 0:BG * D], of))
                dve.sem_inc(st["staged"], 1)

            def gated(i, first, last):
                def x1_of(j):
                    at = BG * D * i + D * j
                    return acc[:, at:at + D] if first or last else acc[:, bass.ds(at, D)]
                x1 = [x1_of(j) for j in range(BG)]
                for j in range(BG + 1):
                    if j < BG:
                        y = ps[4 + j % 2]
                        dve.wait_ge(st["sums"], BG * i + j + 1 + 2)
                        dve.wait_ge(s_ring[j], 32 * (i + 1))
                        V.tensor_tensor(y[:, :], y[:, :], pre_ring[j], ALU.add).then_inc(s_pre, 1)
                    if j == BG - 2 and not last:
                        stage_out(i + 1)
                    if j == 3 and not first:
                        scale(i - 1, [x1_of(j - BG) for j in range(BG)])
                    if j >= 1:
                        n = j - 1
                        h, gate, new = h_ring[:, n, :], gates[:, n % 2, 0:D], gates[:, n % 2, D:2 * D]
                        dve.wait_ge(st["used"], BG * i + n + 1 + 2)
                        own.ordered(V.tensor_tensor(h, h, new, ALU.subtract))
                        own.step(V.tensor_tensor(h, h, gate, ALU.mult))
                        if n:
                            dve.wait_ge(s_mixed, BG * i + n + 2)
                            dve.sem_inc(s_pass, 1)
                            V.bn_stats(stats[:, n - 1, :], x1[n - 1]).then_inc(s_stats, 1)
                        own.settle()
                        dve.wait_ge(s_x1_new, BG * i + n + 1)
                        V.tensor_tensor(x1[n], x1[n], h, ALU.add).then_inc(s_mixed, 1)
                dve.wait_ge(s_mixed, BG * i + BG + 2)
                dve.sem_inc(s_pass, 1)
                V.bn_stats(stats[:, BG - 1, :], x1[BG - 1]).then_inc(s_stats, 1)
                dve.wait_ge(s_stats, BG * i + BG)
                dve.sem_inc(s_pass, 1)
                for j in range(BG):
                    own.step(V.bn_aggr(mv[:, j, :], stats[:, j, :]))
                own.settle()
                dve.sem_inc(st["var"], 1)

            def scale(i, x1):
                dve.wait_ge(st["sd"], i + 1)
                own.ordered(V.reciprocal(rstd[:, :], rstd[:, :]))
                for j in range(BG):
                    own.step(V.tensor_scalar(x1[j], x1[j], mv[:, j, 0:1], rstd[:, j:j + 1],
                                             ALU.subtract, ALU.mult))
                own.settle()
                dve.sem_inc(s_out, 1)
            stage_out(0)
            gated(0, True, False)
            with dve.Fori(1, NG - 1) as i:
                own.loop(i - 1, 1 + 2 * BG + BG + 1 + BG)
                gated(i, False, False)
                own.end(NG - 2)
            gated(NG - 1, False, True)
            scale(NG - 1, [acc[:, BG * D * (NG - 1) + D * j:BG * D * (NG - 1) + D * (j + 1)] for j in range(BG)])


def kernel(x, src, dst, edge_attr_10, edge_attr_4, edge_weight, edge_weight_n2,
           L0_gnn_w_00_0, L0_gnn_w_11_0, L0_gnn_w_01_1, L0_gnn_w_10_1, L0_gnn_fc_w1, L0_gnn_fc_w2,
           L1_gnn_gamma, L1_gnn_beta, L1_gnn_W_in, L1_gnn_b_in, L1_gnn_W_out, L1_gnn_b_out,
           L1_gnn_W_x2i, L1_gnn_b_x2i, L1_gnn_W_h2h):
    import numpy as np
    import concourse.bacc as bacc
    from concourse.bass_utils import run_bass_kernel_spmd

    EP = T0 * P

    def by_lane(a, fill=0):
        a = np.asarray(a)
        whole = np.full((EP,) + a.shape[1:], fill, a.dtype)
        whole[:E] = a
        return whole.reshape(P, -1)

    emb = np.zeros((EP, 10), np.float32)
    emb[:E] = np.asarray(edge_attr_10)
    emb = emb.reshape(P, STEPS, PER, 10).transpose(2, 3, 1, 0)
    dst_t = by_lane(dst, N - 1)
    after = np.concatenate([dst_t[1:, 0], dst_t[-1:, -1]])
    dst_t = np.concatenate([dst_t, after[:, None]], axis=1)
    x_pad = np.zeros((NP, D), np.float32)
    x_pad[:N] = np.asarray(x)
    arrays = {
        "x": x_pad,
        "src_t": by_lane(src, N - 1), "dst_t": dst_t,
        "attr_t": by_lane(edge_attr_4), "iw_t": by_lane(edge_weight), "ow_t": by_lane(edge_weight_n2),
        "emb": emb.reshape(PER * 10, STEPS * P),
        "w00": L0_gnn_w_00_0, "w11": L0_gnn_w_11_0, "w01": L0_gnn_w_01_1, "w10": L0_gnn_w_10_1,
        "fc1": L0_gnn_fc_w1, "fc2": L0_gnn_fc_w2,
        "gamma": np.asarray(L1_gnn_gamma)[None], "beta": np.asarray(L1_gnn_beta)[None],
        "w_in": L1_gnn_W_in, "b_in": np.asarray(L1_gnn_b_in)[None],
        "w_out": L1_gnn_W_out, "b_out": np.asarray(L1_gnn_b_out)[None],
        "w_x2i": L1_gnn_W_x2i, "b_x2i": np.asarray(L1_gnn_b_x2i)[None], "w_h2h": L1_gnn_W_h2h,
    }
    nc = bacc.Bacc("TRN2", target_bir_lowering=False, num_devices=1)
    args, ins = [], {}
    for name, a in arrays.items():
        a = np.ascontiguousarray(np.asarray(a))
        ins["in_" + name] = a
        args.append(nc.dram_tensor("in_" + name, list(a.shape), mybir.dt.from_np(a.dtype),
                                   kind="ExternalInput").ap())
    result = nc.dram_tensor("out_0", [N, D], F32, kind="ExternalOutput").ap()
    build(nc, *args, result)
    r = run_bass_kernel_spmd(nc, [ins], core_ids=[0])
    return r.results[0]["out_0"]
```
